# Optimizing a Trainium2 kernel written in Bass

```python
import numpy as np
import jax
import jax.numpy as jnp

def _softmax(x, axis=-1):
    return jax.nn.softmax(x, axis=axis)

def _gelu(x):
    return jax.nn.gelu(x, approximate=True)

def _silu(x):
    return jax.nn.silu(x)

def _sigmoid(x):
    return jax.nn.sigmoid(x)

def _layernorm(x, axis=-1, eps=1e-05):
    m = jnp.mean(x, axis=axis, keepdims=True)
    v = jnp.var(x, axis=axis, keepdims=True)
    return (x - m) / jnp.sqrt(v + eps)

def _scatter_add(tgt, idx, src, axis=0):
    return tgt.at[idx].add(src)

def _segment_sum(src, seg, n):
    return jax.ops.segment_sum(src, seg, n)
kernel_name = 'mk_prb_d1_jaxref_r8_8be2cf'

def setup_inputs(seed: int=0):
    np.random.seed(seed)
    _w = jnp.asarray

    def _L0_attn_setup():
        import jax, jax.numpy as jnp
        import numpy as np
        N_EMBD = 128
        N_HEAD = 16
        HEAD_DIM = N_EMBD // N_HEAD
        KV_RANK = 32
        Q_RANK = 64
        ROPE_DIM = 32
        B, T = (2, 256)
        EPS = 1e-06

        def _rope_tables(T, dim):
            inv_freq = 1.0 / 10000.0 ** (np.arange(0, dim, 2, dtype=np.float32) / dim)
            t = np.arange(T, dtype=np.float32)
            freqs = np.outer(t, inv_freq)
            emb = np.concatenate([freqs, freqs], -1)
            return (jnp.asarray(np.cos(emb)), jnp.asarray(np.sin(emb)))

        def _apply_rope(x, cos, sin):
            d2 = x.shape[-1] // 2
            x1, x2 = (x[..., :d2], x[..., d2:])
            rot = jnp.concatenate([-x2, x1], axis=-1)
            return x * cos[None, None, :, :] + rot * sin[None, None, :, :]
        key = jax.random.key(seed)
        ks = jax.random.split(key, 10)

        def w(k, fan_in, fan_out):
            return jax.random.normal(k, (fan_in, fan_out), dtype=jnp.float32) * fan_in ** (-0.5)
        return {'x': jax.random.normal(ks[0], (B, T, N_EMBD), dtype=jnp.float32), 'W_kv': w(ks[1], N_EMBD, KV_RANK), 'g_kv': jnp.ones((KV_RANK,), dtype=jnp.float32), 'W_kdec': w(ks[2], KV_RANK, N_HEAD * HEAD_DIM), 'W_vdec': w(ks[3], KV_RANK, N_HEAD * HEAD_DIM), 'W_q': w(ks[4], N_EMBD, Q_RANK), 'W_qdec': w(ks[5], Q_RANK, N_HEAD * HEAD_DIM), 'W_krope': w(ks[6], N_EMBD, N_HEAD * ROPE_DIM), 'W_qrope': w(ks[7], Q_RANK, N_HEAD * ROPE_DIM), 'W_o': w(ks[8], N_HEAD * HEAD_DIM, N_EMBD)}
    _L0_attn_in = _L0_attn_setup()

    def _L0_ffn_setup():
        import jax, jax.numpy as jnp
        import numpy as np
        B, S, H = (2, 256, 128)
        F = 512
        E = 8
        TOP_K = 2
        SHARED_SCALE = 0.1
        EPS = 1e-09

        def _moe_forward(x3, Wg, W1, b1, W2, b2, Ws1, bs1, Ws2, bs2):
            b, s, h = x3.shape
            x = x3.reshape(-1, h)
            T = x.shape[0]
            logits = x @ Wg
            probs = jax.nn.softmax(logits, axis=-1)
            vals, idx = jax.lax.top_k(probs, TOP_K)
            weights = vals / (jnp.sum(vals, axis=-1, keepdims=True) + EPS)
            cw = jnp.zeros((T, E), dtype=x.dtype).at[jnp.arange(T)[:, None], idx].set(weights)
            hpre = jnp.einsum('th,ehf->tef', x, W1) + b1
            act = jax.nn.silu(hpre)
            y = jnp.einsum('tef,efh->teh', act, W2) + b2
            out = jnp.einsum('te,teh->th', cw, y)
            shared = jax.nn.silu(x @ Ws1 + bs1) @ Ws2 + bs2
            out = out + SHARED_SCALE * shared
            return out.reshape(b, s, h)
        key = jax.random.key(seed)
        ks = jax.random.split(key, 10)
        sc = 0.02
        return {'hidden_states': jax.random.normal(ks[0], (B, S, H), dtype=jnp.float32), 'Wg': jax.random.normal(ks[1], (H, E), dtype=jnp.float32) * sc, 'W1': jax.random.normal(ks[2], (E, H, F), dtype=jnp.float32) * sc, 'b1': jnp.zeros((E, F), dtype=jnp.float32), 'W2': jax.random.normal(ks[3], (E, F, H), dtype=jnp.float32) * sc, 'b2': jnp.zeros((E, H), dtype=jnp.float32), 'Ws1': jax.random.normal(ks[4], (H, F), dtype=jnp.float32) * sc, 'bs1': jnp.zeros((F,), dtype=jnp.float32), 'Ws2': jax.random.normal(ks[5], (F, H), dtype=jnp.float32) * sc, 'bs2': jnp.zeros((H,), dtype=jnp.float32)}
    _L0_ffn_in = _L0_ffn_setup()
    _d = {'L0_attn_x': _L0_attn_in['x'], 'L0_attn_W_kv': _L0_attn_in['W_kv'], 'L0_attn_g_kv': _L0_attn_in['g_kv'], 'L0_attn_W_kdec': _L0_attn_in['W_kdec'], 'L0_attn_W_vdec': _L0_attn_in['W_vdec'], 'L0_attn_W_q': _L0_attn_in['W_q'], 'L0_attn_W_qdec': _L0_attn_in['W_qdec'], 'L0_attn_W_krope': _L0_attn_in['W_krope'], 'L0_attn_W_qrope': _L0_attn_in['W_qrope'], 'L0_attn_W_o': _L0_attn_in['W_o'], 'L0_ffn_Wg': _L0_ffn_in['Wg'], 'L0_ffn_W1': _L0_ffn_in['W1'], 'L0_ffn_b1': _L0_ffn_in['b1'], 'L0_ffn_W2': _L0_ffn_in['W2'], 'L0_ffn_b2': _L0_ffn_in['b2'], 'L0_ffn_Ws1': _L0_ffn_in['Ws1'], 'L0_ffn_bs1': _L0_ffn_in['bs1'], 'L0_ffn_Ws2': _L0_ffn_in['Ws2'], 'L0_ffn_bs2': _L0_ffn_in['bs2']}
    _x0 = _d['L0_attn_x']
    _d['L0_attn_x'] = jax.random.normal(jax.random.fold_in(jax.random.key(seed), 1), (16, 256, 128), dtype=_x0.dtype)
    del _x0
    return _d

def reference(L0_attn_x, L0_attn_W_kv, L0_attn_g_kv, L0_attn_W_kdec, L0_attn_W_vdec, L0_attn_W_q, L0_attn_W_qdec, L0_attn_W_krope, L0_attn_W_qrope, L0_attn_W_o, L0_ffn_Wg, L0_ffn_W1, L0_ffn_b1, L0_ffn_W2, L0_ffn_b2, L0_ffn_Ws1, L0_ffn_bs1, L0_ffn_Ws2, L0_ffn_bs2):

    def _L0_attn_ref(x, W_kv, g_kv, W_kdec, W_vdec, W_q, W_qdec, W_krope, W_qrope, W_o):
        import jax, jax.numpy as jnp
        import numpy as np
        N_EMBD = 128
        N_HEAD = 16
        HEAD_DIM = N_EMBD // N_HEAD
        KV_RANK = 32
        Q_RANK = 64
        ROPE_DIM = 32
        B, T = (2, 256)
        EPS = 1e-06

        def _rope_tables(T, dim):
            inv_freq = 1.0 / 10000.0 ** (np.arange(0, dim, 2, dtype=np.float32) / dim)
            t = np.arange(T, dtype=np.float32)
            freqs = np.outer(t, inv_freq)
            emb = np.concatenate([freqs, freqs], -1)
            return (jnp.asarray(np.cos(emb)), jnp.asarray(np.sin(emb)))

        def _apply_rope(x, cos, sin):
            d2 = x.shape[-1] // 2
            x1, x2 = (x[..., :d2], x[..., d2:])
            rot = jnp.concatenate([-x2, x1], axis=-1)
            return x * cos[None, None, :, :] + rot * sin[None, None, :, :]
        Bx, Tx, C = x.shape
        kv_c = x @ W_kv
        kv_c = kv_c * jax.lax.rsqrt(jnp.mean(kv_c * kv_c, axis=-1, keepdims=True) + EPS) * g_kv
        q_c = x @ W_q

        def heads(y, d):
            return y.reshape(Bx, Tx, N_HEAD, d).transpose(0, 2, 1, 3)
        k_content = heads(kv_c @ W_kdec, HEAD_DIM)
        v = heads(kv_c @ W_vdec, HEAD_DIM)
        q_content = heads(q_c @ W_qdec, HEAD_DIM)
        k_rope = heads(x @ W_krope, ROPE_DIM)
        q_rope = heads(q_c @ W_qrope, ROPE_DIM)
        cos, sin = _rope_tables(Tx, ROPE_DIM)
        q_rope = _apply_rope(q_rope, cos, sin)
        k_rope = _apply_rope(k_rope, cos, sin)
        q = jnp.concatenate([q_content, q_rope], axis=-1)
        k = jnp.concatenate([k_content, k_rope], axis=-1)
        scale = 1.0 / jnp.sqrt(jnp.float32(q.shape[-1]))
        scores = jnp.einsum('bhqd,bhkd->bhqk', q, k) * scale
        causal = jnp.tril(jnp.ones((Tx, Tx), dtype=bool))
        scores = jnp.where(causal[None, None], scores, jnp.float32(-jnp.inf))
        attn = jax.nn.softmax(scores, axis=-1)
        out = jnp.einsum('bhqk,bhkd->bhqd', attn, v)
        out = out.transpose(0, 2, 1, 3).reshape(Bx, Tx, N_HEAD * HEAD_DIM)
        return out @ W_o

    def _L0_ffn_ref(hidden_states, Wg, W1, b1, W2, b2, Ws1, bs1, Ws2, bs2):
        import jax, jax.numpy as jnp
        import numpy as np
        B, S, H = (2, 256, 128)
        F = 512
        E = 8
        TOP_K = 2
        SHARED_SCALE = 0.1
        EPS = 1e-09

        def _moe_forward(x3, Wg, W1, b1, W2, b2, Ws1, bs1, Ws2, bs2):
            b, s, h = x3.shape
            x = x3.reshape(-1, h)
            T = x.shape[0]
            logits = x @ Wg
            probs = jax.nn.softmax(logits, axis=-1)
            vals, idx = jax.lax.top_k(probs, TOP_K)
            weights = vals / (jnp.sum(vals, axis=-1, keepdims=True) + EPS)
            cw = jnp.zeros((T, E), dtype=x.dtype).at[jnp.arange(T)[:, None], idx].set(weights)
            hpre = jnp.einsum('th,ehf->tef', x, W1) + b1
            act = jax.nn.silu(hpre)
            y = jnp.einsum('tef,efh->teh', act, W2) + b2
            out = jnp.einsum('te,teh->th', cw, y)
            shared = jax.nn.silu(x @ Ws1 + bs1) @ Ws2 + bs2
            out = out + SHARED_SCALE * shared
            return out.reshape(b, s, h)
        return _moe_forward(hidden_states, Wg, W1, b1, W2, b2, Ws1, bs1, Ws2, bs2)
    x = L0_attn_x
    xn = _layernorm(x, axis=-1)
    x = x + _L0_attn_ref(xn, L0_attn_W_kv, L0_attn_g_kv, L0_attn_W_kdec, L0_attn_W_vdec, L0_attn_W_q, L0_attn_W_qdec, L0_attn_W_krope, L0_attn_W_qrope, L0_attn_W_o) + _L0_ffn_ref(xn, L0_ffn_Wg, L0_ffn_W1, L0_ffn_b1, L0_ffn_W2, L0_ffn_b2, L0_ffn_Ws1, L0_ffn_bs1, L0_ffn_Ws2, L0_ffn_bs2)
    return x

_drawn_inputs = setup_inputs


def setup_inputs(seed=0):
    import zlib

    import numpy as np

    out = dict(_drawn_inputs(seed))
    spreads = {'L0_attn_g_kv': (1.0, 0.2),
     'L0_ffn_b1': (0.0, 0.504),
     'L0_ffn_b2': (0.0, 0.1),
     'L0_ffn_bs1': (0.0, 0.8),
     'L0_ffn_bs2': (0.0, 0.8)}
    factors = {'L0_ffn_Ws1': 8.0, 'L0_ffn_Ws2': 8.0}
    for name, (base, spread) in spreads.items():
        noise = np.random.default_rng([zlib.crc32(name.encode()), seed]).standard_normal(out[name].shape)
        drawn = base * np.exp(spread * noise) if base else spread * noise
        out[name] = jnp.asarray(drawn.astype(out[name].dtype))
    for name, factor in factors.items():
        out[name] = (out[name] * factor).astype(out[name].dtype)
    return out
```

```python
from contextlib import ExitStack

import concourse.bass as bass
from concourse import mybir

F32 = mybir.dt.float32
F32R = mybir.dt.float32r
BF16 = mybir.dt.bfloat16
ALU = mybir.AluOpType
ACT = mybir.ActivationFunctionType
AX = mybir.AxisListType

P = 128
B, T, C = 16, 256, 128
NT = T // P
TILES = B * NT
H, DC, DR = 16, 8, 32
D = DC + DR
HD = H * DC
RKV, RQ = 32, 64
E, F = 8, 512
FC = F // P
NE = E + 1
SCALE = float(D) ** -0.5
NEG = -1.0e30
KQ = 3 * D
KK = KQ + 2
GH = H // 2
GW = GH * DC
SMW = RKV + RQ + E
DIAG = P + DC
LN_EPS, RMS_EPS, TOP_EPS = 1e-5, 1e-6, 1e-9
SMALL_STEPS, ROT_STEPS = 13, 2 * (4 + 2)
INIT = 1 + NT * 2 + NT + 5

STEPS = H
SHIFT = 4
PV_LAG = 2
FILLS = {1: (0, 1, 2), 2: (3, 4, 5), 3: (6, 7, 8), 4: (9, 10, 11), 5: (12, 13, 14), 6: (15,)}
S_AT = {7: (0, 1), 8: (2, 3), 9: (4, 5), 10: (6, 7), 11: (8, 9), 12: (10, 11), 13: (12, 13), 14: (14,), 15: (15,)}
MT_STEP = 1
PROJ_AT = {4: ("q", 0), 6: ("k", 0), 8: ("q", 1), 10: ("k", 1)}
LOW_AT = {7: 0, 11: 1}
XT_STEP, SM_STEP, QK_STEP = 11, 13, 15
WO_STEP = SHIFT + PV_LAG + 2

FILLS_N = 16
B_UNITS = FILLS_N + H + 1
B_FREES = (FILLS_N + H) // 2
PROJ_UNITS = 4 * NT


FILL_OF = [(0, 0, 0), (0, 0, 4), (0, 0, 8), (0, 1, 0), (0, 1, 4), (0, 1, 8), (1, 0, 0), (1, 0, 4), (1, 0, 8),
           (0, 0, 12), (0, 1, 12), (1, 1, 0), (1, 1, 4), (1, 1, 8), (1, 0, 12), (1, 1, 12)]


def fills_until(j, side, h0):
    return FILL_OF.index((j, side, h0)) + 1


def at_least(eng, sem, value):
    if isinstance(value, int) and value <= 0:
        return
    eng.wait_ge(sem, value)


def known(b, last=B - 1):
    return not isinstance(b, int) or 0 <= b <= last


class Chain:

    def __init__(self, eng, sem, b, per_batch):
        self.eng, self.sem, self.b, self.per, self.n = eng, sem, b, per_batch, 0

    def add(self, ins):
        self.n += 1
        ins.then_inc(self.sem, 1)
        return self.n

    def need(self, n=None):
        self.eng.wait_ge(self.sem, self.b * self.per + (self.n if n is None else n))


def build(nc, x, W_kv, g_kv, W_kdec, W_vdec, W_q, W_qdec, W_krope, W_qrope, W_o,
          Wg, W1, b1, W2, b2, Ws1, bs1, Ws2, bs2, rope, out):
    x_d = x.rearrange("b (j p) c -> p (b j) c", p=P)
    out_d = out.rearrange("b (j p) c -> p (b j) c", p=P)
    parts_d = nc.dram_tensor("xn_parts", (P, 2, B * T), F32R).ap()

    with ExitStack() as ctx:
        def sb(name, shape, dt):
            return ctx.enter_context(nc.sbuf_tensor(name, shape, dt))

        def sem(name):
            return ctx.enter_context(nc.semaphore(name))

        xres = sb("xres", [P, TILES, C], F32)
        lg = sb("lg", [P, TILES, E], F32)
        w2 = sb("w2", [P, NE, FC, C], F32)
        w1raw = sb("w1raw", [P, E, F], F32)
        bias1 = sb("bias1", [P, NE * FC], F32)
        b2x = sb("b2x", [NE, C], F32)
        wo = sb("wo", [HD, C], F32)
        wsm = sb("wsm", [P, 2 * P], F32R)
        wkr = sb("wkr", [P, 2, H * DR], F32R)
        wqa = sb("wqa", [2 * RQ, H, D], F32R)
        wqb = sb("wqb", [2 * RQ, H, D], F32R)
        wkv = sb("wkv", [3 * RKV, 2 * HD], F32R)
        ident = sb("ident", [P, P], F32)
        identr = sb("identr", [P, P], F32R)
        identb = sb("identb", [P, P], BF16)
        mask_qk = sb("mask_qk", [P, P], BF16)
        mask_kq = sb("mask_kq", [P, P], BF16)
        cosx = sb("cosx", [P, NT, D], F32)
        sins = sb("sins", [P, NT, DR], F32)
        QK = sb("QK", [P, 2, 2, H, T], F32R)
        stk = {(s, j): sb(f"stk_{s}{j}", [P, H, KQ if s == "q" else KK], F32R)
               for s in "qk" for j in range(NT)}
        vpad = sb("vpad", [P, NT * H * P + P], F32)
        vraw = sb("vraw", [P, 2, NT, HD], F32)
        prob = sb("prob", [P, 4, 3 * P], F32)
        r = {s: sb(f"rot_{s}", [P, H, D], F32) for s in "qk"}
        t2 = sb("t2", [P, H, DR], F32)
        st6 = sb("st6", [P, NT, 6], F32)
        mv = sb("mv", [P, NT, 2], F32)
        rstd = sb("rstd", [P, NT], F32)
        mhalf = sb("mhalf", [P, NT], F32)
        unit = sb("unit", [P, GH], F32)
        pace = sb("pace", [P, 1], F32)
        xn = sb("xn", [P, NT, C], F32)
        xhl = sb("xhl", [P, 2, 2, T], F32R)
        smt = sb("smt", [P, NT, SMW], F32)
        sq = sb("sq", [P, NT, RKV], F32)
        ss = sb("ss", [P, NT], F32)
        rs = sb("rs", [P, NT], F32)
        kvn = sb("kvn", [P, NT, RKV], F32)
        qs = sb("qs", [P, NT, 2, RQ], F32R)
        ks = sb("ks", [P, NT, 3, RKV], F32R)
        qsT = sb("qsT", [2 * RQ, NT, P], F32R)
        ksT = sb("ksT", [3 * RKV, NT, P], F32R)
        mx = sb("mx", [P, NT, H], F32)
        nhl = sb("nhl", [P, NT, 2, H], F32R)
        mT = sb("mT", [2 * H, T], F32R)
        numden = sb("numden", [P, 2, T], F32)
        num, den = numden[:, 0, :], numden[:, 1, :]
        oT = sb("oT", [P, T], F32)
        cw = sb("cw", [P, TILES, NE], F32)
        rsm = sb("rsm", [P, 3, TILES], F32)
        cwc = sb("cwc", [P, 2, 4, NE], F32)

        raw_kr = r["q"][:, :, :].rearrange("p h d -> p (h d)")[:, 0:H * DR]
        raw_qr = r["k"][:, :, :].rearrange("p h d -> p (h d)")[:, 0:H * DR]
        raw_sm = t2[:, :, :].rearrange("p h d -> p (h d)")[:, 0:SMW]
        raw_qd = t2[:, :, :].rearrange("p h d -> p (h d)")[:, P:P + HD]
        raw_kv = t2[0:3 * RKV, :, :].rearrange("p h d -> p (h d)")[:, 2 * P:2 * P + 2 * HD]
        g_rep = sq[0:3 * RKV, 0, 0:1]
        kv_hi = qs[0:3 * RKV, :, :, :].rearrange("p j a r -> p (j a r)")
        braw = numden[0:NE * FC, 0, 0:P]

        w1p = QK[:, 0, :, :, :].rearrange("p a h t -> p a (h t)")[:, :, 0:E * F]
        act = vpad[:, 0:2 * FC * 4 * P].rearrange("p (n c t) -> p n c t", n=2, c=FC)
        xc = [stk["q", n][:, :, :].rearrange("p h k -> p (h k)")[:, 0:2 * 4 * P]
              .rearrange("p (a t) -> p a t", a=2) for n in range(2)]
        ws1 = stk["k", 0][:, :, :].rearrange("p h k -> p (h k)")[:, 0:2 * F].rearrange("p (a f) -> p a f", a=2)
        ws1raw = numden[:, :, :].rearrange("p a t -> p (a t)")
        cwT = prob[:, :, :].rearrange("p n k -> p (n k)")[0:NE, 0:4 * P]
        flat = lambda t: t[:, :, :].rearrange("p h d -> p (h d)")
        cmp_gt = flat(r["q"])[:, 0:8 * E * E].rearrange("p (i a c) -> p i a c", a=E, c=E)
        cmp_eq = flat(r["k"])[:, 0:8 * E * E].rearrange("p (i a c) -> p i a c", a=E, c=E)
        pr = flat(t2)[:, 0:TILES * E].rearrange("p (i e) -> p i e", e=E)
        rank = flat(t2)[:, TILES * E:2 * TILES * E].rearrange("p (i e) -> p i e", e=E)
        tri8 = sb("tri8", [P, E, E], BF16)

        banks = [ctx.enter_context(nc.psum_tensor(f"bank{i}", [P, 512], F32)) for i in range(8)]
        A_PS, B_PS, ST_PS, PV_PS = banks[0:2], banks[2:4], banks[4:6], banks[6:8]


        def diagonal(start):
            return vpad[:, start:start + GH * DIAG].rearrange("p (h c) -> p h c", c=DIAG)[:, :, 0:DC]

        def w1_part(e, part, start, n):
            return w1p[:, part, e * F + start:e * F + start + n] if e < E else ws1[:, part, start:start + n]

        N_X = 4
        XL = TILES // N_X
        s_x = [sem(f"x{n}_loaded") for n in range(N_X)]
        s_wa = sem("attention_weights_loaded")
        s_wm = sem("expert_weights_loaded")
        s_const = sem("constants_built")
        s_cast = sem("identities_cast")
        s_init = sem("buffers_preset")
        s_wsplit = sem("attention_weights_split")
        s_biasT = sem("expert_bias_turned")
        s_bias = sem("expert_bias_ready")
        s_xn = sem("xn_ready")
        s_var = sem("variance_ready")
        s_rstd = sem("deviation_inverted")
        s_ms = sem("mean_square_ready")
        s_rs = sem("mean_square_inverted")
        s_xh = sem("xn_high_ready")
        s_xl = sem("xn_low_ready")
        s_xst = [sem(f"xn_parts{i}_stored") for i in range(2)]
        s_smh = sem("small_high_read")
        s_small = sem("small_stacks_ready")
        s_smT = sem("small_stacks_turned")
        s_afill = sem("small_bank_filled")
        s_pfill = sem("projection_bank_filled")
        s_pfree = [sem(f"projection_bank{i}_free") for i in range(2)]
        s_bfill = sem("stack_bank_filled")
        s_bfree = [sem(f"stack_bank{i}_free") for i in range(2)]
        s_rot = {s: sem(f"rotated_{s}") for s in "qk"}
        s_kc = sem("key_content_ready")
        s_v = sem("values_ready")
        s_hi = {s: sem(f"high_{s}_stacked") for s in "qk"}
        s_lo = {s: sem(f"low_{s}_stacked") for s in "qk"}
        s_nm = sem("negative_max_ready")
        s_mT = sem("max_rows_ready")
        s_mrow = sem("max_rows_placed")
        s_st = sem("scores_done")
        s_exp = sem("probs_ready")
        s_pv = sem("head_values_done")
        s_vp = sem("values_placed")
        s_ev = sem("group_values_read")
        s_oT = sem("attention_normed")
        s_wo = sem("attention_projected")
        s_acc = sem("attention_added")
        c_a = sem("dve_small_steps")
        c_r = sem("dve_rotation_steps")
        c_b = sem("dve_first_tile_maxima")
        c_n = sem("dve_negative_max_high")
        c_c = sem("dve_sum_inverted")
        c_s = sem("dve_setup_steps")
        s_w1h = sem("w1_high_ready")
        s_w1l = sem("w1_low_ready")
        s_ws = sem("shared_weights_loaded")
        c_rt = sem("dve_router_steps")
        s_rt = sem("router_logits_less_max")
        s_exr = sem("router_exp_ready")
        s_cw = sem("chunk_weights_ready")
        s_xc = [sem(f"xn_chunk{i}_loaded") for i in range(2)]
        s_l1 = sem("hidden_done")
        s_act = [sem(f"activation{c}_ready") for c in range(FC)]
        s_l2 = [sem(f"expert_out{i}_done") for i in range(2)]
        s_comb = [sem(f"expert_out{i}_added") for i in range(2)]
        c_m = sem("dve_combine_steps")
        s_cwt = sem("chunk_weights_turned")
        s_cwe = sem("chunk_weights_turned_read")
        s_b2 = sem("bias2_done")
        s_b2a = sem("bias2_added")
        s_out = sem("out_stored")

        block = ctx.enter_context(nc.Block())

        CHUNKS = TILES // 4
        WA_LOADS = 4 + 4 + 9 + 3
        WM_LOADS = 7

        def run_turns(eng, body):
            for b in (-3, -2, -1, 0, 1):
                body(b, b % 2)
            with eng.Fori(1, 6) as g:
                for par in range(2):
                    body(g * 2 + par, par)
            for b in (12, 13, 14, 15, 16):
                body(b, b % 2)

        def run_chunks(eng, body):
            body(0)
            with eng.Fori(1, CHUNKS // 2) as g:
                body(g)

        def stored_before(b, par):
            return 8 * (b - par)

        def scores_of(b, s):
            return (b, s - SHIFT) if s >= SHIFT else (b - 1, s - SHIFT + H)

        def values_of(b, s):
            return (b, s - SHIFT - PV_LAG) if s >= SHIFT + PV_LAG else (b - 1, s - SHIFT - PV_LAG + H)

        @block.sync
        def _(sp):
            sp.dma_start(xres[:, 0:XL, :], x_d[:, 0:XL, :]).then_inc(s_x[0], 16)
            sp.dma_start(raw_sm[:, 0:RKV], W_kv).then_inc(s_wa, 16)
            sp.dma_start(raw_sm[:, RKV:RKV + RQ], W_q).then_inc(s_wa, 16)
            sp.dma_start(raw_sm[:, RKV + RQ:SMW], Wg).then_inc(s_wa, 16)
            sp.dma_start(raw_kr, W_krope).then_inc(s_wa, 16)
            for n in range(2):
                sp.dma_start(raw_qr[n * RQ:(n + 1) * RQ, :], W_qrope).then_inc(s_wa, 16)
                sp.dma_start(raw_qd[n * RQ:(n + 1) * RQ, :], W_qdec).then_inc(s_wa, 16)
            for n in range(3):
                rows = slice(n * RKV, (n + 1) * RKV)
                sp.dma_start(raw_kv[rows, 0:HD], W_kdec).then_inc(s_wa, 16)
                sp.dma_start(raw_kv[rows, HD:2 * HD], W_vdec).then_inc(s_wa, 16)
                sp.dma_start(g_rep[rows, :], g_kv.rearrange("(r a) -> r a", a=1)).then_inc(s_wa, 16)
            sp.dma_start(wo[:, :], W_o).then_inc(s_wa, 16)
            rope_v = rope.rearrange("(j p) c -> p j c", p=P)
            sp.dma_start(cosx[:, :, :], rope_v[:, :, 0:D]).then_inc(s_wa, 16)
            sp.dma_start(sins[:, :, :], rope_v[:, :, D:D + DR]).then_inc(s_wa, 16)
            for n in range(1, N_X):
                sp.dma_start(xres[:, n * XL:(n + 1) * XL, :], x_d[:, n * XL:(n + 1) * XL, :]).then_inc(s_x[n], 16)
            sp.dma_start(braw[0:E * FC, :], b1.rearrange("e (c p) -> (e c) p", p=P)).then_inc(s_wm, 16)
            sp.dma_start(braw[E * FC:NE * FC, :], bs1.rearrange("(c p) -> c p", p=P)).then_inc(s_wm, 16)
            sp.dma_start(w1raw[:, 0:E, :], W1.rearrange("e h f -> h e f")).then_inc(s_wm, 16)
            sp.dma_start(w2[:, 0:E, :, :], W2.rearrange("e (c p) h -> p e c h", p=P)).then_inc(s_wm, 16)
            sp.dma_start(w2[:, E, :, :], Ws2.rearrange("(c p) h -> p c h", p=P)).then_inc(s_wm, 16)
            sp.dma_start(b2x[0:E, :], b2).then_inc(s_wm, 16)
            sp.dma_start(b2x[E:NE, :], bs2.rearrange("(a h) -> a h", a=1)).then_inc(s_wm, 16)

            def turn(b, par):
                if known(b):
                    sp.wait_ge(s_mT, b + 1)
                    sp.dma_start(QK[KQ:KK, par, 0, :, :].bitcast(F32), mT[:, :].bitcast(F32)).then_inc(s_mrow, 16)
                if known(b + 3):
                    at = slice((b + 3) * T, (b + 4) * T) if isinstance(b, int) else bass.ds(sp.snap((b + 3) * T), T)
                    sp.wait_ge(s_xh, b + 4)
                    sp.wait_ge(s_xl, b + 4)
                    sp.wait_ge(s_x[0], 16)
                    sp.dma_start(parts_d[:, :, at].bitcast(F32), xhl[:, (par + 1) % 2, :, :].bitcast(F32)).then_inc(s_xst[(par + 1) % 2], 16)

            run_turns(sp, turn)

            sp.wait_ge(s_acc, B)
            sp.dma_start(ws1raw, Ws1).then_inc(s_ws, 16)
            for i in range(2):
                sp.wait_ge(s_xst[i], 8 * B)
            sp.wait_ge(s_bfill, B * B_UNITS)

            def load_chunk(n, at):
                sp.dma_start(xc[n].bitcast(F32), parts_d[:, :, at].bitcast(F32)).then_inc(s_xc[n], 16)

            def store_chunk(g, n):
                m = (n + 1) * NE - 1
                at = slice((2 * g + n) * 4, (2 * g + n + 1) * 4) if isinstance(g, int) else \
                    bass.ds(sp.snap(g * 8 + 4 * n), 4)
                sp.wait_ge(s_comb[m % 2], g * NE + m // 2 + 1)
                sp.wait_ge(s_x[0], 16)
                sp.dma_start(out_d[:, at, :], xres[:, at, :]).then_inc(s_out, 16)

            for n in range(2):
                load_chunk(n, slice(n * 4 * P, (n + 1) * 4 * P))
            with sp.Fori(0, CHUNKS // 2 - 1) as g:
                for n in range(2):
                    store_chunk(g, n)
                    at = bass.ds(sp.snap((g * 2 + n + 2) * (4 * P)), 4 * P)
                    sp.wait_ge(s_l1, (g * 2 + n + 1) * (NE * FC))
                    sp.wait_ge(s_x[0], 16)
                    load_chunk(n, at)
            for n in range(2):
                store_chunk(CHUNKS // 2 - 1, n)
            sp.wait_ge(s_out, 16 * CHUNKS)

        @block.gpsimd
        def _(pool):
            nc.gpsimd.memset(ident[:, :], 0.0).then_inc(s_const, 1)
            nc.gpsimd.memset(mask_qk[:, :], 0.0).then_inc(s_const, 1)
            nc.gpsimd.memset(mask_kq[:, :], 0.0).then_inc(s_const, 1)
            nc.gpsimd.memset(tri8[:, :, :], 1.0).then_inc(s_const, 1)
            pool.wait_ge(s_const, 4)
            nc.gpsimd.affine_select(out=ident[:, :], in_=ident[:, :], compare_op=ALU.not_equal, fill=1.0,
                                    base=0, pattern=[[-1, P]], channel_multiplier=1).then_inc(s_const, 1)
            nc.gpsimd.affine_select(out=mask_qk[:, :], in_=mask_qk[:, :], compare_op=ALU.is_ge, fill=NEG,
                                    base=0, pattern=[[-1, P]], channel_multiplier=1).then_inc(s_const, 1)
            nc.gpsimd.affine_select(out=mask_kq[:, :], in_=mask_kq[:, :], compare_op=ALU.is_ge, fill=NEG,
                                    base=0, pattern=[[1, P]], channel_multiplier=-1).then_inc(s_const, 1)
            nc.gpsimd.affine_select(out=tri8[:, :, :], in_=tri8[:, :, :], compare_op=ALU.is_gt, fill=0.0,
                                    base=0, pattern=[[1, E], [-1, E]], channel_multiplier=0).then_inc(s_const, 1)
            nc.gpsimd.memset(vpad[:, :], 0.0).then_inc(s_init, 1)
            pool.wait_ge(s_init, 1)
            for n in range(NT * 2):
                ones = diagonal(n * GH * P + GW)
                nc.gpsimd.memset(ones, 1.0).then_inc(s_init, 1)
            for j in range(NT):
                nc.gpsimd.memset(stk["k", j][:, :, KQ:KK].bitcast(F32), 1.0).then_inc(s_init, 1)
            nc.gpsimd.memset(wsm[:, :].bitcast(F32), 0.0).then_inc(s_init, 1)
            nc.gpsimd.memset(wqb[:, :, :].bitcast(F32), 0.0).then_inc(s_init, 1)
            nc.gpsimd.memset(cw[:, :, E:NE], 0.1).then_inc(s_init, 1)
            nc.gpsimd.memset(mhalf[:, :], -0.5).then_inc(s_init, 1)
            nc.gpsimd.memset(unit[:, :], 1.0).then_inc(s_init, 1)
            pool.wait_ge(s_init, INIT)

            def turn(b, par):
                if known(b + 3):
                    pool.wait_ge(s_var, b + 4)
                    nc.gpsimd.tensor_tensor(rstd[:, :], rstd[:, :], mhalf[:, :], ALU.pow).then_inc(s_rstd, 1)
                    pool.wait_ge(s_ms, b + 4)
                    nc.gpsimd.tensor_tensor(rs[:, :], rs[:, :], mhalf[:, :], ALU.pow).then_inc(s_rs, 1)

            def place(b, par):
                for bb, g, pp in ((b, 0, par), (b, 1, par)):
                    if known(bb):
                        pool.wait_ge(s_v, NT * (bb + 1))
                        at_least(pool, s_pv, (bb - 1) * H + (g + 1) * GH)
                        for j in range(NT):
                            ins = nc.gpsimd.tensor_tensor(
                                diagonal((j * H + g * GH) * P),
                                vraw[:, pp, j, g * GW:(g + 1) * GW].rearrange("p (h d) -> p h d", d=DC),
                                unit[:, :].unsqueeze(2).to_broadcast([P, GH, DC]), ALU.mult)
                            ins.then_inc(s_vp, 1)

            def whole(b, par):
                place(b, par)
                turn(b, par)

            run_turns(pool, whole)

        @block.scalar
        def _(sc):
            act_f = nc.scalar.activation
            sc.wait_ge(s_const, 8)
            act_f(identr[:, :], ident[:, :], ACT.Copy).then_inc(s_cast, 1)
            act_f(identb[:, :], ident[:, :], ACT.Copy).then_inc(s_cast, 1)
            sc.wait_ge(s_biasT, 1)
            act_f(bias1[:, :], banks[1][:, 0:NE * FC], ACT.Copy).then_inc(s_bias, 1)

            def turn(b, par):
                for s in range(STEPS):
                    bb, h = scores_of(b, s)
                    if known(bb):
                        n = bb * H + h
                        sc.wait_ge(s_st, n + 1)
                        at_least(sc, s_pv, n - 3)
                        act_f(prob[:, h % 4, :], ST_PS[h % 2][:, 0:3 * P], ACT.Exp, scale=SCALE).then_inc(s_exp, 1)
                    bb, h = values_of(b, s)
                    if known(bb) and h % GH == GH - 1:
                        g = h // GH
                        rows = slice(g * GW, (g + 1) * GW)
                        sc.wait_ge(s_pv, bb * H + h + 1)
                        at_least(sc, s_oT, bb)
                        act_f(num[rows], PV_PS[g][0:GW, 0:T], ACT.Copy).then_inc(s_ev, 1)
                        act_f(den[rows], PV_PS[g][GW:2 * GW, 0:T], ACT.Copy).then_inc(s_ev, 1)
                    if s == MT_STEP and known(b):
                        sc.wait_ge(s_bfill, (b + 1) * B_UNITS)
                        at_least(sc, s_mrow, 16 * b)
                        act_f(mT[:, :], B_PS[0][0:2 * H, 0:T], ACT.Copy).then_inc(s_mT, 1)
                    if known(b + 1):
                        for f in FILLS.get(s, ()):
                            j, side, h0 = FILL_OF[f]
                            rows = KK if side else KQ
                            sc.wait_ge(s_bfill, (b + 1) * B_UNITS + f + 1)
                            at_least(sc, s_st, (b - 1) * H + h0 + 4)
                            act_f(QK[0:rows, (par + 1) % 2, side, h0:h0 + 4, j * P:(j + 1) * P],
                                  B_PS[f % 2][0:rows, :].rearrange("p (h t) -> p h t", h=4),
                                  ACT.Copy).then_inc(s_bfree[f % 2], 1)
                    if known(b + 2) and s in PROJ_AT:
                        side, j = PROJ_AT[s]
                        n = (b + 2) * NT + j
                        if side == "k":
                            sc.wait_ge(s_pfill, (b + 2) * PROJ_UNITS + 4 * j + 4)
                            at_least(sc, s_vp, 2 * NT * (b + 1))
                            act_f(vraw[:, par, j, :], banks[0][:, HD:2 * HD], ACT.Copy).then_inc(s_v, 1)
                            at_least(sc, s_lo["k"], n)
                            act_f(r["k"][:, :, 0:DC], banks[0][:, 0:HD].rearrange("p (h d) -> p h d", h=H),
                                  ACT.Copy).then_inc(s_pfree[0], 1)
                            sc.wait_ge(s_pfree[0], (b + 2) * 4 + 2 * j + 2)
                        sc.wait_ge(s_rot[side], n + 1)
                        at_least(sc, s_bfill, (b + 1) * B_UNITS + fills_until(j, "qk".index(side), 12) if known(b + 1) else 0)
                        src = r[side][:, :, :].unsqueeze(2).to_broadcast([P, H, 2, D])
                        dst = stk[side, j][:, :, 0:KQ].rearrange("p h (a d) -> p h a d", a=3)
                        dst = dst[:, :, 0:2, :] if side == "q" else dst[:, :, 0:3:2, :]
                        act_f(dst, src, ACT.Copy).then_inc(s_hi[side], 1)
                    if known(b + 3) and s == XT_STEP:
                        sc.wait_ge(s_afill, (b + 3) * 3 + 1)
                        at_least(sc, s_xst[(par + 1) % 2], stored_before(b + 3, (par + 1) % 2))
                        at_least(sc, s_pfill, (b + 2) * PROJ_UNITS)
                        act_f(xhl[:, (par + 1) % 2, 0, :], banks[0][:, 0:T], ACT.Copy).then_inc(s_xh, 1)
                    if known(b + 3) and s == SM_STEP:
                        sc.wait_ge(s_afill, (b + 3) * 3 + 2)
                        at_least(sc, s_small, b + 3)
                        act_f(smt[:, :, :], banks[1][:, :].rearrange("p (j c) -> p j c", j=NT)[:, :, 0:SMW],
                              ACT.Copy).then_inc(s_smh, 1)
                    if known(b + 3) and s == QK_STEP:
                        sc.wait_ge(s_afill, (b + 3) * 3 + 3)
                        at_least(sc, s_pfill, (b + 3) * PROJ_UNITS)
                        act_f(qsT[:, :, :], banks[0][:, 0:T].rearrange("p (j t) -> p j t", j=NT),
                              ACT.Copy).then_inc(s_smT, 1)
                        act_f(ksT[:, :, :], banks[0][0:3 * RKV, T:2 * T].rearrange("p (j t) -> p j t", j=NT),
                              ACT.Copy).then_inc(s_smT, 1)
                    if isinstance(b, int) and b == B - 1:
                        if s == 2:
                            sc.wait_ge(s_rt, 1)
                            act_f(pr, pr, ACT.Exp).then_inc(s_exr, 1)
                        if 5 <= s < 5 + E:
                            e = s - 5
                            if e == 0:
                                sc.wait_ge(s_wm, 16 * WM_LOADS)
                                sc.wait_ge(s_st, (B - 1) * H)
                            act_f(w1_part(e, 0, 0, F), w1raw[:, e, :], ACT.Copy).then_inc(s_w1h, 1)

            run_turns(sc, turn)

            sc.wait_ge(s_ws, 16)
            act_f(w1_part(E, 0, 0, F), ws1raw, ACT.Copy).then_inc(s_w1h, 1)

            def chunks(g):
                for n in range(2):
                    sc.wait_ge(s_cwt, g * 2 + n + 1)
                    act_f(cwT[:, :], banks[7][0:NE, :], ACT.Copy).then_inc(s_cwe, 1)
                    for e in range(NE):
                        m = n * NE + e
                        for c in range(FC):
                            k = e * FC + c
                            sc.wait_ge(s_l1, g * (2 * NE * FC) + m * FC + c + 1)
                            if c == 0:
                                at_least(sc, s_l2[m % 2], g * NE + m // 2)
                            act_f(act[:, m % 2, c, :], banks[c][:, :], ACT.Silu,
                                  bias=bias1[:, k:k + 1]).then_inc(s_act[c], 1)

            run_chunks(sc, chunks)

        @block.vector
        def _(dve):
            V = nc.vector

            steps = Chain(dve, c_s, 0, 0)
            dve.wait_ge(s_wa, 16 * WA_LOADS)
            dve.wait_ge(s_init, INIT)
            steps.add(V.tensor_scalar(raw_kv, raw_kv, g_rep, None, ALU.mult))
            steps.add(V.tensor_copy(wsm[:, 0:SMW], raw_sm))
            steps.add(V.tensor_copy(wkr[:, 0, :], raw_kr))
            steps.add(V.tensor_copy(wqa[:, :, 0:DC], raw_qd.rearrange("p (h d) -> p h d", h=H)))
            steps.add(V.tensor_copy(wqa[:, :, DC:D], raw_qr.rearrange("p (h d) -> p h d", h=H)))
            steps.need()
            steps.add(V.tensor_copy(kv_hi, raw_kv))
            steps.add(V.tensor_tensor(wsm[:, P:P + SMW], raw_sm, wsm[:, 0:SMW], ALU.subtract))
            steps.add(V.tensor_tensor(wkr[:, 1, :], raw_kr, wkr[:, 0, :], ALU.subtract))
            steps.add(V.tensor_tensor(wqb[0:RQ, :, 0:DC], raw_qd[0:RQ, :].rearrange("p (h d) -> p h d", h=H),
                                      wqa[0:RQ, :, 0:DC], ALU.subtract))
            steps.add(V.tensor_tensor(wqb[0:RQ, :, DC:D], raw_qr[0:RQ, :].rearrange("p (h d) -> p h d", h=H),
                                      wqa[0:RQ, :, DC:D], ALU.subtract))
            steps.need()
            steps.add(V.tensor_copy(wkv[0:2 * RKV, :], raw_kv[0:2 * RKV, :]))
            steps.need()
            V.tensor_tensor(wkv[2 * RKV:3 * RKV, :], raw_kv[2 * RKV:3 * RKV, :], kv_hi[2 * RKV:3 * RKV, :],
                            ALU.subtract).then_inc(s_wsplit, 1)
            dve.wait_ge(s_wsplit, 1)

            def normalise(b, steps):
                i = b * NT
                at_least(dve, c_a, b * SMALL_STEPS)
                at_least(dve, s_xn, b * NT)
                for n in range(N_X):
                    if not isinstance(b, int) or n == i // XL:
                        dve.wait_ge(s_x[n], 16)
                for j in range(NT):
                    at = slice(i + j, i + j + 1) if isinstance(b, int) else bass.ds(i + j, 1)
                    steps.add(V.bn_stats(st6[:, j, :], xres[:, at, :]))
                steps.need()
                steps.add(V.memset(pace[:, :], 0.0))
                for j in range(NT):
                    steps.add(V.bn_aggr(mv[:, j, :], st6[:, j, :]))
                steps.need()
                V.tensor_scalar(rstd[:, :], mv[:, :, 1], LN_EPS, None, ALU.add).then_inc(s_var, 1)

            def normalised(b):
                i = b * NT
                dve.wait_ge(s_rstd, b + 1)
                at_least(dve, s_afill, 3 * b - 2)
                for j in range(NT):
                    at = slice(i + j, i + j + 1) if isinstance(b, int) else bass.ds(i + j, 1)
                    V.tensor_scalar(xn[:, j:j + 1, :], xres[:, at, :], mv[:, j, 0:1], rstd[:, j:j + 1],
                                    ALU.subtract, ALU.mult).then_inc(s_xn, 1)

            def small_products(b, steps):
                low = banks[1][:, :].rearrange("p (j c) -> p j c", j=NT)
                dve.wait_ge(s_smh, b + 1)
                at = slice(b * NT, (b + 1) * NT) if isinstance(b, int) else bass.ds(b * NT, NT)
                steps.add(V.tensor_tensor(lg[:, at, :], low[:, :, P + RKV + RQ:P + SMW], smt[:, :, RKV + RQ:SMW], ALU.add))
                steps.add(V.tensor_tensor(smt[:, :, 0:RKV + RQ], low[:, :, P:P + RKV + RQ],
                                          smt[:, :, 0:RKV + RQ], ALU.add))
                steps.need()
                kv, qc = smt[:, :, 0:RKV], smt[:, :, RKV:RKV + RQ]
                steps.add(V.tensor_tensor(sq[:, :, :], kv, kv, ALU.mult))
                at_least(dve, s_afill, 3 * b)
                steps.add(V.tensor_copy(qs[:, :, 0, :], qc))
                steps.need()
                steps.add(V.tensor_reduce(ss[:, :], sq[:, :, :], AX.X, ALU.add))
                steps.need()
                V.tensor_scalar(rs[:, :], ss[:, :], 1.0 / RKV, RMS_EPS, ALU.mult, ALU.add).then_inc(s_ms, 1)

            def small_stacks(b, steps):
                kv, qc = smt[:, :, 0:RKV], smt[:, :, RKV:RKV + RQ]
                dve.wait_ge(s_rs, b + 1)
                steps.add(V.tensor_tensor(kvn[:, :, :], kv, rs[:, :].unsqueeze(2).to_broadcast([P, NT, RKV]), ALU.mult))
                steps.need()
                steps.add(V.tensor_copy(ks[:, :, 0:3:2, :], kvn[:, :, :].unsqueeze(2).to_broadcast([P, NT, 2, RKV])))
                steps.need()
                steps.add(V.tensor_tensor(ks[:, :, 1, :], kvn[:, :, :], ks[:, :, 0, :], ALU.subtract))
                V.tensor_tensor(qs[:, :, 1, :], qc, qs[:, :, 0, :], ALU.subtract).then_inc(s_small, 1)

            def rotate(b, side, j, steps):
                n = b * NT + j
                out = r[side]
                at_least(dve, s_hi[side], n)
                at_least(dve, s_lo[side], n)
                at_least(dve, s_rot["k" if side == "q" else "q"], n if side == "q" else n + 1)
                if side == "q":
                    for half in range(2):
                        hs = slice(half * GH, (half + 1) * GH)
                        bank = 1 - half
                        dve.wait_ge(s_pfill, b * PROJ_UNITS + 4 * j + half + 1)
                        ps = banks[bank][:, 0:GH * D].rearrange("p (h d) -> p h d", h=GH)
                        steps.add(V.tensor_tensor(out[:, hs, :], ps,
                                                  cosx[:, j, :].unsqueeze(1).to_broadcast([P, GH, D]), ALU.mult))
                        turned(ps[:, :, DC:D], hs, j, steps, bank)
                else:
                    dve.wait_ge(s_pfill, b * PROJ_UNITS + 4 * j + 3)
                    ps = banks[1][:, :].rearrange("p (h d) -> p h d", h=H)
                    steps.add(V.tensor_tensor(out[:, :, DC:D], ps,
                                              cosx[:, j, DC:D].unsqueeze(1).to_broadcast([P, H, DR]), ALU.mult))
                    turned(ps, slice(0, H), j, steps, 1)
                steps.need()
                dve.wait_ge(s_pfree[1], b * 4 + 2 * j + (1 if side == "q" else 2))
                if side == "q":
                    dve.wait_ge(s_pfree[0], b * 4 + 2 * j + 1)
                V.tensor_tensor(out[:, :, DC:D], out[:, :, DC:D], t2[:, :, :], ALU.add).then_inc(s_rot[side], 1)

            def turned(ps, hs, j, steps, bank):
                hh, n = DR // 2, hs.stop - hs.start
                steps.add(V.tensor_tensor(t2[:, hs, 0:hh], ps[:, :, hh:DR],
                                          sins[:, j, 0:hh].unsqueeze(1).to_broadcast([P, n, hh]), ALU.mult))
                V.tensor_tensor(t2[:, hs, hh:DR], ps[:, :, 0:hh],
                                sins[:, j, hh:DR].unsqueeze(1).to_broadcast([P, n, hh]), ALU.mult)\
                    .then_inc(s_pfree[bank], 1)

            def low_part(b, side, j):
                dve.wait_ge(s_hi[side], b * NT + j + 1)
                st = stk[side, j]
                slot = slice(2 * D, 3 * D) if side == "q" else slice(D, 2 * D)
                V.tensor_tensor(st[:, :, slot], r[side][:, :, :], st[:, :, 0:D], ALU.subtract).then_inc(s_lo[side], 1)

            def router():
                steps = Chain(dve, c_rt, 0, 0)
                bc = lambda t: t.unsqueeze(2).to_broadcast([P, TILES, E])
                top, tot, inv = rsm[:, 0, :], rsm[:, 1, :], rsm[:, 2, :]
                dve.wait_ge(c_a, B * SMALL_STEPS)
                for side in "qk":
                    dve.wait_ge(s_rot[side], TILES)
                    dve.wait_ge(s_hi[side], TILES)
                    dve.wait_ge(s_lo[side], TILES)
                steps.add(V.tensor_reduce(top, lg[:, :, :], AX.X, ALU.max))
                steps.need()
                V.tensor_tensor(pr, lg[:, :, :], bc(top), ALU.subtract).then_inc(s_rt, 1)
                dve.wait_ge(s_exr, 1)
                steps.add(V.tensor_reduce(tot, pr, AX.X, ALU.add))
                steps.need()
                steps.add(V.reciprocal(inv, tot))
                steps.need()
                steps.add(V.tensor_tensor(pr, pr, bc(inv), ALU.mult))
                steps.need()
                for q in range(TILES // 8):
                    ts = slice(8 * q, 8 * q + 8)
                    mine = pr[:, ts, :].unsqueeze(3).to_broadcast([P, 8, E, E])
                    other = pr[:, ts, :].unsqueeze(2).to_broadcast([P, 8, E, E])
                    steps.add(V.tensor_tensor(cmp_gt, other, mine, ALU.is_gt))
                    steps.add(V.tensor_tensor(cmp_eq, other, mine, ALU.is_equal))
                    steps.need()
                    steps.add(V.tensor_tensor(cmp_eq, cmp_eq, tri8[:, :, :].unsqueeze(1).to_broadcast([P, 8, E, E]), ALU.mult))
                    steps.need()
                    steps.add(V.tensor_tensor(cmp_gt, cmp_gt, cmp_eq, ALU.add))
                    steps.need()
                    steps.add(V.tensor_reduce(rank[:, ts, :], cmp_gt, AX.X, ALU.add))
                    steps.need()
                steps.add(V.tensor_scalar(rank, rank, 2.0, None, ALU.is_lt))
                steps.need()
                steps.add(V.tensor_tensor(pr, pr, rank, ALU.mult))
                steps.need()
                steps.add(V.tensor_reduce(tot, pr, AX.X, ALU.add))
                steps.need()
                steps.add(V.tensor_scalar(tot, tot, TOP_EPS, None, ALU.add))
                steps.need()
                steps.add(V.reciprocal(inv, tot))
                steps.need()
                steps.add(V.tensor_tensor(cw[:, :, 0:E], pr, bc(inv), ALU.mult))
                steps.need()

            def turn(b, par):
                small = Chain(dve, c_a, b + 3, SMALL_STEPS)
                rot = Chain(dve, c_r, b + 2, ROT_STEPS)
                for s in range(STEPS):
                    if known(b - 1) and s == SHIFT + PV_LAG:
                        dve.wait_ge(s_ev, 4 * b)
                        V.reciprocal(den, den).then_inc(c_c, 1)
                        dve.wait_ge(c_c, b)
                        at_least(dve, s_wo, b - 1)
                        V.tensor_tensor(oT[:, :], num, den, ALU.mult).then_inc(s_oT, 1)
                    if known(b - 1) and s == WO_STEP + 1:
                        dve.wait_ge(s_wo, b)
                        at = slice((b - 1) * NT, b * NT) if isinstance(b, int) else bass.ds((b - 1) * NT, NT)
                        V.tensor_tensor(xres[:, at, :], PV_PS[1][:, 0:T].rearrange("p (j c) -> p j c", j=NT),
                                        xres[:, at, :], ALU.add).then_inc(s_acc, 1)
                    if known(b + 1):
                        for h in S_AT.get(s, ()):
                            dve.wait_ge(s_bfill, (b + 1) * B_UNITS + FILLS_N + h + 1)
                            ps = B_PS[h % 2]
                            V.tensor_reduce(mx[:, 0, h:h + 1], ps[:, 0:P], AX.X, ALU.max).then_inc(c_b, 1)
                            V.tensor_reduce(mx[:, 1, h:h + 1], ps[:, T:2 * T], AX.X, ALU.max).then_inc(s_bfree[h % 2], 1)
                        if s == max(S_AT):
                            dve.wait_ge(c_b, (b + 2) * H)
                            for i in range(2):
                                dve.wait_ge(s_bfree[i], (b + 2) * B_FREES)
                            at_least(dve, s_bfill, (b + 1) * B_UNITS)
                            V.tensor_scalar(nhl[:, :, 0, :], mx[:, :, :], -1.0, None, ALU.mult).then_inc(c_n, 1)
                            dve.wait_ge(c_n, b + 2)
                            V.scalar_tensor_tensor(out=nhl[:, :, 1, :], in0=mx[:, :, :], scalar=-1.0,
                                                   in1=nhl[:, :, 0, :], op0=ALU.mult, op1=ALU.subtract).then_inc(s_nm, 1)
                    if known(b + 2):
                        if s in PROJ_AT:
                            side, j = PROJ_AT[s]
                            rotate(b + 2, side, j, rot)
                            if side == "k":
                                low_part(b + 2, "q", j)
                        if s in LOW_AT:
                            low_part(b + 2, "k", LOW_AT[s])
                    if known(b + 3):
                        if s == XT_STEP - 2:
                            normalise(b + 3, small)
                        if s == XT_STEP - 1:
                            normalised(b + 3)
                        if s == XT_STEP:
                            dve.wait_ge(s_xh, b + 4)
                            V.tensor_tensor(xhl[:, (par + 1) % 2, 1, :], banks[0][:, 0:T], xhl[:, (par + 1) % 2, 0, :],
                                            ALU.subtract).then_inc(s_xl, 1)
                        if s == SM_STEP:
                            small_products(b + 3, small)
                        if s == SM_STEP + 1:
                            small_stacks(b + 3, small)
                    if isinstance(b, int) and b == B - 1:
                        if s == 0:
                            router()
                        if 5 <= s < 5 + E:
                            e = s - 5
                            dve.wait_ge(s_w1h, e + 1)
                            V.tensor_tensor(w1_part(e, 1, 0, F), w1raw[:, e, :], w1_part(e, 0, 0, F),
                                            ALU.subtract).then_inc(s_w1l, 1)
                assert not known(b + 3) or small.n == SMALL_STEPS, small.n
                assert not known(b + 2) or rot.n == ROT_STEPS, rot.n

            run_turns(dve, turn)

            dve.wait_ge(s_w1h, NE)
            V.tensor_tensor(w1_part(E, 1, 0, F), ws1raw, w1_part(E, 0, 0, F), ALU.subtract).then_inc(s_w1l, 1)
            dve.wait_ge(s_acc, B)

            def chunks(g):
                for n in range(2):
                    for i in range(2):
                        at_least(dve, s_comb[i], g * NE)
                    at_least(dve, c_m, g * (2 * NE * 3))
                    chunk = bass.ds(g * 8 + 4 * n, 4)
                    V.tensor_copy(cwc[:, n, :, :], cw[:, chunk, :]).then_inc(s_cw, 1)
                    dve.wait_ge(s_cw, g * 2 + n + 1)
                    dve.wait_ge(s_b2, g * 2 + n + 1)
                    V.tensor_tensor(xres[:, chunk, :], banks[6][:, :].rearrange("p (i c) -> p i c", i=4),
                                    xres[:, chunk, :], ALU.add).then_inc(s_b2a, 1)
                    dve.wait_ge(s_b2a, g * 2 + n + 1)
                    for e in range(NE):
                        m = n * NE + e
                        dve.wait_ge(s_l2[m % 2], g * NE + m // 2 + 1)
                        if e:
                            dve.wait_ge(c_m, (g * 2 * NE + m) * 3)
                            dve.wait_ge(s_comb[(m - 1) % 2], g * NE + (m - 1) // 2 + 1)
                        for i in range(4):
                            tile = xres[:, bass.ds(g * 8 + 4 * n + i, 1), :].squeeze(1)
                            V.scalar_tensor_tensor(out=tile, in0=banks[4 + m % 2][:, i * P:(i + 1) * P],
                                                   scalar=cwc[:, n, i, e:e + 1], in1=tile, op0=ALU.mult,
                                                   op1=ALU.add).then_inc(c_m if i < 3 else s_comb[m % 2], 1)

            run_chunks(dve, chunks)

        @block.tensor
        def _(pe):
            mm = nc.tensor.matmul
            pe.wait_ge(s_const, 8)
            pe.wait_ge(s_wm, 16 * WM_LOADS)
            nc.tensor.transpose(banks[1][:, 0:NE * FC], braw, ident[0:NE * FC, 0:NE * FC]).then_inc(s_biasT, 1)
            pe.wait_ge(s_cast, 2)
            pe.wait_ge(s_bias, 1)
            pe.wait_ge(s_wsplit, 1)

            def head_scores(b, h, par):
                ps, n = ST_PS[h % 2], b * H + h
                q, k = QK[0:KK, par, 0, h, :], QK[0:KK, par, 1, h, :]
                if h == 0:
                    pe.wait_ge(s_mrow, 16 * (b + 1))
                at_least(pe, s_exp, n - 1)
                mm(ps[:, P:3 * P], k[:, P:T], q, start=True, stop=False, skip_group_check=True)
                mm(ps[:, T:3 * P], identb[:, :], mask_kq[:, :], start=False, stop=True, skip_group_check=True)
                mm(ps[:, 0:T], k[:, 0:P], q, start=True, stop=False, skip_group_check=True)
                mm(ps[:, 0:P], identb[:, :], mask_kq[:, :], start=False, stop=True,
                   skip_group_check=True).then_inc(s_st, 1)

            def head_values(b, h):
                g, ps = h // GH, PV_PS[h // GH]
                if h % GH == 0:
                    pe.wait_ge(s_vp, (2 * b + g + 1) * NT)
                    at_least(pe, s_ev, 4 * b - 2 + 2 * g)
                    if g == 1:
                        at_least(pe, s_acc, b)
                pe.wait_ge(s_exp, b * H + h + 1)
                p = prob[:, h % 4, :]
                mm(ps[:, 0:T], vpad[:, h * P:(h + 1) * P], p[:, 0:T], start=(h % GH == 0), stop=False)
                mm(ps[:, P:T], vpad[:, (H + h) * P:(H + h + 1) * P], p[:, T:3 * P],
                   start=False, stop=(h % GH == GH - 1)).then_inc(s_pv, 1)

            def output_projection(b):
                pe.wait_ge(s_oT, b + 1)
                for j in range(NT):
                    ins = mm(PV_PS[1][:, j * P:(j + 1) * P], oT[:, j * P:(j + 1) * P], wo[:, :], start=True, stop=True)
                ins.then_inc(s_wo, 1)

            def turn_stacks(b, f):
                j, side, h0 = FILL_OF[f]
                rows = KK if side else KQ
                if h0 == 0:
                    pe.wait_ge(s_lo["qk"[side]], b * NT + j + 1)
                at_least(pe, s_bfree[f % 2], b * B_FREES + f // 2)
                if f == 0:
                    at_least(pe, s_mT, b)
                for i in range(4):
                    ins = nc.tensor.transpose(B_PS[f % 2][0:rows, i * P:(i + 1) * P].bitcast(F32R),
                                              stk["qk"[side], j][:, h0 + i, 0:rows], identr[:, :])
                ins.then_inc(s_bfill, 1)

            def scores_for_max(b, h, par):
                ps = B_PS[h % 2]
                q, k = QK[0:KQ, par, 0, h, :], QK[0:KQ, par, 1, h, :]
                for i in range(2):
                    if i == h % 2 or h == 0:
                        pe.wait_ge(s_bfree[i], b * B_FREES + FILLS_N // 2 + h // 2)
                mm(ps[:, 0:T], q[:, 0:P], k, start=True, stop=False, skip_group_check=True)
                mm(ps[:, T:2 * T], q[:, P:T], k, start=False, stop=False, skip_group_check=True)
                diag = ps[:, :].rearrange("p (a c) -> p a c", a=4)[:, 0:4:3, :]
                mm(diag, identb[:, :], mask_qk[:, :].unsqueeze(1).to_broadcast([P, 2, P]), start=False, stop=True,
                   skip_group_check=True).then_inc(s_bfill, 1)

            def turn_maxima(b):
                pe.wait_ge(s_nm, b + 1)
                pe.wait_ge(s_bfree[0], (b + 1) * B_FREES)
                for j in range(NT):
                    ins = nc.tensor.transpose(B_PS[0][0:2 * H, j * P:(j + 1) * P].bitcast(F32R),
                                              nhl[:, j, :, :].rearrange("p a h -> p (a h)"), identr[:, :])
                ins.then_inc(s_bfill, 1)

            def project(b, side, j, par):
                k0 = b * 4 + 2 * j
                qrow, kvrow = qsT[:, j, :], ksT[:, j, :]
                xh, xl = (xhl[:, par, a, j * P:(j + 1) * P] for a in range(2))
                pe.wait_ge(s_smT, 2 * (b + 1))
                if side == "q":
                    for half in range(2):
                        bank = 1 - half
                        at_least(pe, s_pfree[bank], k0)
                        hs = slice(half * GH, (half + 1) * GH)
                        ps = banks[bank][:, 0:GH * D]
                        mm(ps, qrow, wqa[:, hs, :].rearrange("p h d -> p (h d)"), start=True, stop=False)
                        mm(ps, qrow, wqb[:, hs, :].rearrange("p h d -> p (h d)"), start=False, stop=True)\
                            .then_inc(s_pfill, 1)
                else:
                    pe.wait_ge(s_pfree[1], k0 + 1)
                    mm(banks[1][:, :], xh, wkr[:, 0, :], start=True, stop=False)
                    mm(banks[1][:, :], xl, wkr[:, 0, :], start=False, stop=False)
                    mm(banks[1][:, :], xh, wkr[:, 1, :], start=False, stop=True).then_inc(s_pfill, 1)
                    pe.wait_ge(s_pfree[0], k0 + 1)
                    mm(banks[0][:, 0:2 * HD], kvrow, wkv[:, :], start=True, stop=True).then_inc(s_pfill, 1)

            def turn(b, par):
                for s in range(STEPS):
                    bb, h = scores_of(b, s)
                    if known(bb):
                        head_scores(bb, h, par if s >= SHIFT else (par + 1) % 2)
                    bb, h = values_of(b, s)
                    if known(bb):
                        head_values(bb, h)
                    if s == MT_STEP and known(b):
                        turn_maxima(b)
                    if s == WO_STEP and known(b - 1):
                        output_projection(b - 1)
                    if known(b + 1):
                        for f in FILLS.get(s, ()):
                            turn_stacks(b + 1, f)
                        for h in S_AT.get(s, ()):
                            scores_for_max(b + 1, h, (par + 1) % 2)
                    if known(b + 2) and s in PROJ_AT:
                        project(b + 2, *PROJ_AT[s], par)
                    if known(b + 3):
                        if s == XT_STEP:
                            pe.wait_ge(s_xn, NT * (b + 4))
                            at_least(pe, s_pfree[0], 4 * (b + 3))
                            for j in range(NT):
                                ins = nc.tensor.transpose(banks[0][:, j * P:(j + 1) * P], xn[:, j, :], ident[:, :])
                            ins.then_inc(s_afill, 1)
                        if s == SM_STEP:
                            pe.wait_ge(s_xl, b + 4)
                            at_least(pe, s_pfree[1], 4 * (b + 3))
                            for j in range(NT):
                                for a in range(2):
                                    ins = mm(banks[1][:, j * T:(j + 1) * T],
                                             xhl[:, (par + 1) % 2, a, j * P:(j + 1) * P], wsm[:, :],
                                             start=(a == 0), stop=(a == 1))
                            ins.then_inc(s_afill, 1)
                        if s == QK_STEP:
                            pe.wait_ge(s_small, b + 4)
                            for j in range(NT):
                                nc.tensor.transpose(banks[0][:, j * P:(j + 1) * P].bitcast(F32R),
                                                    qs[:, j, :, :].rearrange("p a r -> p (a r)"), identr[:, :])
                            for j in range(NT):
                                ins = nc.tensor.transpose(banks[0][0:3 * RKV, (NT + j) * P:(NT + j + 1) * P].bitcast(F32R),
                                                          ks[:, j, :, :].rearrange("p a r -> p (a r)"), identr[:, :])
                            ins.then_inc(s_afill, 1)

            run_turns(pe, turn)

            for i in range(2):
                pe.wait_ge(s_pfree[i], 4 * B)
                pe.wait_ge(s_bfree[i], B_FREES * B)
            pe.wait_ge(s_exp, H * B)
            pe.wait_ge(s_ev, 4 * B)
            pe.wait_ge(s_acc, B)

            def hidden(g, n, e):
                m = n * NE + e
                if n == 0 and e in (0, E):
                    pe.wait_ge(s_w1l, E if e == 0 else NE)
                if e == 0:
                    pe.wait_ge(s_xc[n], (g + 1) * 16)
                for c in range(FC):
                    at_least(pe, s_act[c], g * (2 * NE) + m)
                    for i, (w, a) in enumerate(((0, 0), (0, 1), (1, 0))):
                        ins = mm(banks[c][:, :], w1_part(e, w, c * P, P), xc[n][:, a, :], start=(i == 0), stop=(i == 2))
                    ins.then_inc(s_l1, 1)

            def expert_out(g, n, e):
                m = n * NE + e
                pe.wait_ge(s_act[FC - 1], g * (2 * NE) + m + 1)
                at_least(pe, s_comb[m % 2], g * NE + m // 2)
                for i in range(4):
                    for c in range(FC):
                        ins = mm(banks[4 + m % 2][:, i * P:(i + 1) * P], act[:, m % 2, c, i * P:(i + 1) * P],
                                 w2[:, e, c, :], start=(c == 0), stop=(c == FC - 1))
                ins.then_inc(s_l2[m % 2], 1)

            def chunks(g):
                for n in range(2):
                    hidden(g, n, 0)
                    pe.wait_ge(s_cw, g * 2 + n + 1)
                    for i in range(4):
                        ins = nc.tensor.transpose(banks[7][0:NE, i * P:(i + 1) * P], cwc[:, n, i, :], ident[:, :])
                    ins.then_inc(s_cwt, 1)
                    hidden(g, n, 1)
                    pe.wait_ge(s_cwe, g * 2 + n + 1)
                    at_least(pe, s_b2a, g * 2 + n)
                    for i in range(4):
                        ins = mm(banks[6][:, i * P:(i + 1) * P], cwT[:, i * P:(i + 1) * P], b2x[:, :], start=True, stop=True)
                    ins.then_inc(s_b2, 1)
                    for e in range(NE):
                        if 2 <= e + 1 < NE:
                            hidden(g, n, e + 1)
                        expert_out(g, n, e)

            run_chunks(pe, chunks)


_INS = ['L0_attn_x', 'L0_attn_W_kv', 'L0_attn_g_kv', 'L0_attn_W_kdec', 'L0_attn_W_vdec', 'L0_attn_W_q',
        'L0_attn_W_qdec', 'L0_attn_W_krope', 'L0_attn_W_qrope', 'L0_attn_W_o', 'L0_ffn_Wg', 'L0_ffn_W1',
        'L0_ffn_b1', 'L0_ffn_W2', 'L0_ffn_b2', 'L0_ffn_Ws1', 'L0_ffn_bs1', 'L0_ffn_Ws2', 'L0_ffn_bs2']


def rope_table(np):
    inv_freq = 1.0 / 10000.0 ** (np.arange(0, DR, 2, dtype=np.float32) / DR)
    freqs = np.outer(np.arange(T, dtype=np.float32), inv_freq)
    cos, sin = np.cos(freqs), np.sin(freqs)
    return np.concatenate([np.ones((T, DC)), cos, cos, -sin, sin], -1).astype(np.float32)


def kernel(**inputs):
    import numpy as np
    import concourse.bacc as bacc
    from concourse.bass_utils import run_bass_kernel_spmd

    nc = bacc.Bacc("TRN2", target_bir_lowering=False, num_devices=1)
    arrays, args = {}, []
    for name in _INS:
        a = np.ascontiguousarray(inputs[name])
        arrays[f"in_{name}"] = a
        args.append(nc.dram_tensor(f"in_{name}", a.shape, mybir.dt.from_np(a.dtype), kind="ExternalInput").ap())
    table = rope_table(np)
    arrays["in_rope"] = table
    args.append(nc.dram_tensor("in_rope", table.shape, F32, kind="ExternalInput").ap())
    args.append(nc.dram_tensor("out", (B, T, C), F32, kind="ExternalOutput").ap())
    build(nc, *args)
    r = run_bass_kernel_spmd(nc, [arrays], core_ids=[0])
    return r.results[0]["out"]
```

```python
from contextlib import ExitStack

import concourse.bass as bass
from concourse import mybir

F32 = mybir.dt.float32
F32R = mybir.dt.float32r
BF16 = mybir.dt.bfloat16
ALU = mybir.AluOpType
ACT = mybir.ActivationFunctionType
AX = mybir.AxisListType

P = 128
B, T, C = 16, 256, 128
NT = T // P
TILES = B * NT
H, DC, DR = 16, 8, 32
D = DC + DR
HD = H * DC
RKV, RQ = 32, 64
E, F = 8, 512
FC = F // P
NE = E + 1
SCALE = float(D) ** -0.5
NEG = -1.0e30
KQ = 3 * D
KK = KQ + 2
GH = H // 2
GW = GH * DC
SMW = RKV + RQ + E
DIAG = P + DC
LN_EPS, RMS_EPS, TOP_EPS = 1e-5, 1e-6, 1e-9
SMALL_STEPS, ROT_STEPS = 13, 2 * (4 + 2)
INIT = 1 + NT * 2 + NT + 5

STEPS = H
SHIFT = 4
PV_LAG = 2
UNITS_AT = {
    1: (("t", 0, "q", 0), ("t", 0, "q", 4)), 2: (("t", 0, "q", 8), ("t", 1, "q", 0)),
    3: (("t", 0, "q", 12), ("t", 1, "q", 4)), 4: (("t", 1, "q", 8), ("t", 1, "q", 12)),
    5: (("t", 0, "k", 0), ("t", 0, "k", 4)), 6: (("t", 0, "k", 8), ("t", 0, "k", 12)),
    7: (("t", 1, "k", 0), ("t", 1, "k", 4)), 8: (("t", 1, "k", 8), ("t", 1, "k", 12)),
    9: (("s", 0), ("s", 1), ("s", 2)), 10: (("s", 3), ("s", 4)), 11: (("s", 5), ("s", 6), ("s", 7)),
    12: (("s", 8), ("s", 9)), 13: (("s", 10), ("s", 11)), 14: (("s", 12), ("s", 13)), 15: (("s", 14), ("s", 15))}
UNITS = [u for s in sorted(UNITS_AT) for u in UNITS_AT[s]]
MT_STEP = 1
PROJ_AT = {1: ("q", 0), 3: ("q", 1), 5: ("k", 0), 7: ("k", 1)}
ROT_AT = {s + 1: what for s, what in PROJ_AT.items()}
HIGH_AT = {s + 2: what for s, what in PROJ_AT.items()}
XT_STEP, SM_STEP, QK_STEP = 9, 11, 15
WO_STEP = SHIFT + PV_LAG + 2

B_UNITS = len(UNITS) + 1
B_FREES = len(UNITS) // 2
PROJ_UNITS = 4 * NT


def units_until(what):
    return UNITS.index(what) + 1


def by_dve(what):
    return any(what == UNITS_AT[s][1] for s in (1, 3, 5, 7))


def order_of(side, j):
    return list(PROJ_AT.values()).index((side, j))


def bank_of(what):
    return units_until(what) % 2


def uses_until(what, bank):
    return (units_until(what) + bank) // 2


def at_least(eng, sem, value):
    if isinstance(value, int) and value <= 0:
        return
    eng.wait_ge(sem, value)


def known(b, last=B - 1):
    return not isinstance(b, int) or 0 <= b <= last


class Chain:

    def __init__(self, eng, sem, b, per_batch):
        self.eng, self.sem, self.b, self.per, self.n = eng, sem, b, per_batch, 0

    def add(self, ins):
        self.n += 1
        ins.then_inc(self.sem, 1)
        return self.n

    def need(self, n=None):
        self.eng.wait_ge(self.sem, self.b * self.per + (self.n if n is None else n))


def build(nc, x, W_kv, g_kv, W_kdec, W_vdec, W_q, W_qdec, W_krope, W_qrope, W_o,
          Wg, W1, b1, W2, b2, Ws1, bs1, Ws2, bs2, rope, out):
    x_d = x.rearrange("b (j p) c -> p (b j) c", p=P)
    out_d = out.rearrange("b (j p) c -> p (b j) c", p=P)
    parts_d = nc.dram_tensor("xn_parts", (P, 2, B * T), F32R).ap()

    with ExitStack() as ctx:
        def sb(name, shape, dt):
            return ctx.enter_context(nc.sbuf_tensor(name, shape, dt))

        def sem(name):
            return ctx.enter_context(nc.semaphore(name))

        xres = sb("xres", [P, TILES, C], F32)
        lg = sb("lg", [P, TILES, E], F32)
        w2 = sb("w2", [P, NE, FC, C], F32)
        w1raw = sb("w1raw", [P, E, F], F32)
        bias1 = sb("bias1", [P, NE * FC], F32)
        b2x = sb("b2x", [NE, C], F32)
        wo = sb("wo", [HD, C], F32)
        wsm = sb("wsm", [P, 2 * P], F32R)
        wkr = sb("wkr", [P, 2, H * DR], F32R)
        wqa = sb("wqa", [2 * RQ, H, D], F32R)
        wqb = sb("wqb", [2 * RQ, H, D], F32R)
        wkv = sb("wkv", [3 * RKV, 2 * HD], F32R)
        ident = sb("ident", [P, P], F32)
        identr = sb("identr", [P, P], F32R)
        identb = sb("identb", [P, P], BF16)
        mask_qk = sb("mask_qk", [P, P], BF16)
        mask_kq = sb("mask_kq", [P, P], BF16)
        cosx = sb("cosx", [P, NT, D], F32)
        sins = sb("sins", [P, NT, DR], F32)
        QK = sb("QK", [P, 2, 2, H, T], F32R)
        stk = {(s, j): sb(f"stk_{s}{j}", [P, H, KQ if s == "q" else KK], F32R)
               for s in "qk" for j in range(NT)}
        vpad = sb("vpad", [P, NT * H * P + P], F32)
        vraw = sb("vraw", [P, 2, NT, HD], F32)
        prob = sb("prob", [P, 4, 3 * P], F32)
        r = {s: sb(f"rot_{s}", [P, H, D], F32) for s in "qk"}
        t2 = sb("t2", [P, H, DR], F32)
        st6 = sb("st6", [P, NT, 6], F32)
        mv = sb("mv", [P, NT, 2], F32)
        rstd = sb("rstd", [P, NT], F32)
        mhalf = sb("mhalf", [P, NT], F32)
        unit = sb("unit", [P, H], F32)
        pace = sb("pace", [P, 1], F32)
        xn = sb("xn", [P, NT, C], F32)
        xhl = sb("xhl", [P, 2, 2, T], F32R)
        smt = sb("smt", [P, NT, SMW], F32)
        sq = sb("sq", [P, NT, RKV], F32)
        ss = sb("ss", [P, NT], F32)
        rs = sb("rs", [P, NT], F32)
        qs = sb("qs", [P, NT, 2, RQ], F32R)
        ks = sb("ks", [P, NT, 3, RKV], F32R)
        qsT = sb("qsT", [2 * RQ, NT, P], F32R)
        ksT = sb("ksT", [3 * RKV, NT, P], F32R)
        mx = sb("mx", [P, NT, H], F32)
        nhl = sb("nhl", [P, NT, 2, H], F32R)
        mT = sb("mT", [2 * H, T], F32R)
        numden = sb("numden", [P, 2, T], F32)
        num, den = numden[:, 0, :], numden[:, 1, :]
        oT = sb("oT", [P, T], F32)
        cw = sb("cw", [P, TILES, NE], F32)
        rsm = sb("rsm", [P, 3, TILES], F32)
        cwc = sb("cwc", [P, 2, 4, NE], F32)

        raw_kr = r["q"][:, :, :].rearrange("p h d -> p (h d)")[:, 0:H * DR]
        raw_qr = r["k"][:, :, :].rearrange("p h d -> p (h d)")[:, 0:H * DR]
        raw_sm = t2[:, :, :].rearrange("p h d -> p (h d)")[:, 0:SMW]
        raw_qd = t2[:, :, :].rearrange("p h d -> p (h d)")[:, P:P + HD]
        raw_kv = t2[0:3 * RKV, :, :].rearrange("p h d -> p (h d)")[:, 2 * P:2 * P + 2 * HD]
        g_rep = sq[0:3 * RKV, 0, 0:1]
        kv_hi = qs[0:3 * RKV, :, :, :].rearrange("p j a r -> p (j a r)")
        braw = numden[0:NE * FC, 0, 0:P]

        w1p = QK[:, 0, :, :, :].rearrange("p a h t -> p a (h t)")[:, :, 0:E * F]
        act = vpad[:, 0:2 * FC * 4 * P].rearrange("p (n c t) -> p n c t", n=2, c=FC)
        xc = [stk["q", n][:, :, :].rearrange("p h k -> p (h k)")[:, 0:2 * 4 * P]
              .rearrange("p (a t) -> p a t", a=2) for n in range(2)]
        ws1 = stk["k", 0][:, :, :].rearrange("p h k -> p (h k)")[:, 0:2 * F].rearrange("p (a f) -> p a f", a=2)
        ws1raw = numden[:, :, :].rearrange("p a t -> p (a t)")
        cwT = prob[:, :, :].rearrange("p n k -> p (n k)")[0:NE, 0:4 * P]
        flat = lambda t: t[:, :, :].rearrange("p h d -> p (h d)")
        cmp_gt = flat(r["q"])[:, 0:8 * E * E].rearrange("p (i a c) -> p i a c", a=E, c=E)
        cmp_eq = flat(r["k"])[:, 0:8 * E * E].rearrange("p (i a c) -> p i a c", a=E, c=E)
        pr = flat(t2)[:, 0:TILES * E].rearrange("p (i e) -> p i e", e=E)
        rank = flat(t2)[:, TILES * E:2 * TILES * E].rearrange("p (i e) -> p i e", e=E)
        tri8 = sb("tri8", [P, E, E], BF16)

        banks = [ctx.enter_context(nc.psum_tensor(f"bank{i}", [P, 512], F32)) for i in range(8)]
        A_PS, B_PS, ST_PS, PV_PS = banks[0:2], banks[2:4], banks[4:6], banks[6:8]


        def diagonal(start):
            return vpad[:, start:start + GH * DIAG].rearrange("p (h c) -> p h c", c=DIAG)[:, :, 0:DC]

        def w1_part(e, part, start, n):
            return w1p[:, part, e * F + start:e * F + start + n] if e < E else ws1[:, part, start:start + n]

        N_X = 4
        XL = TILES // N_X
        s_x = [sem(f"x{n}_loaded") for n in range(N_X)]
        s_wa = sem("attention_weights_loaded")
        s_wm = sem("expert_weights_loaded")
        s_const = sem("constants_built")
        s_cast = sem("identities_cast")
        s_init = sem("buffers_preset")
        s_wsplit = sem("attention_weights_split")
        s_biasT = sem("expert_bias_turned")
        s_bias = sem("expert_bias_ready")
        s_xn = sem("xn_ready")
        s_var = sem("variance_ready")
        s_rstd = sem("deviation_inverted")
        s_ms = sem("mean_square_ready")
        s_rs = sem("mean_square_inverted")
        s_xh = sem("xn_high_ready")
        s_xl = sem("xn_low_ready")
        s_xst = [sem(f"xn_parts{i}_stored") for i in range(2)]
        s_smh = sem("small_high_read")
        s_small = sem("small_stacks_ready")
        s_smT = sem("small_stacks_turned")
        s_afill = sem("small_bank_filled")
        s_pfill = sem("projection_bank_filled")
        s_pfree = [sem(f"projection_bank{i}_free") for i in range(2)]
        s_bfill = sem("stack_bank_filled")
        s_bfree = [sem(f"stack_bank{i}_free") for i in range(2)]
        s_rot = {s: sem(f"rotated_{s}") for s in "qk"}
        s_kc = sem("key_content_ready")
        s_v = sem("values_ready")
        s_hi = {s: sem(f"high_{s}_stacked") for s in "qk"}
        s_dup = {s: sem(f"high_{s}_stacked_again") for s in "qk"}
        s_lo = {s: sem(f"low_{s}_stacked") for s in "qk"}
        s_nm = sem("negative_max_ready")
        s_mT = sem("max_rows_ready")
        s_mrow = sem("max_rows_placed")
        s_st = sem("scores_done")
        s_exp = sem("probs_ready")
        s_pv = sem("head_values_done")
        s_vp = sem("values_placed")
        s_ev = sem("group_values_read")
        s_oT = sem("attention_normed")
        s_wo = sem("attention_projected")
        s_acc = sem("attention_added")
        c_a = sem("dve_small_steps")
        c_r = sem("dve_rotation_steps")
        c_b = sem("dve_first_tile_maxima")
        c_n = sem("dve_negative_max_high")
        c_c = sem("dve_sum_inverted")
        c_s = sem("dve_setup_steps")
        s_w1h = sem("w1_high_ready")
        s_w1l = sem("w1_low_ready")
        s_ws = sem("shared_weights_loaded")
        c_rt = sem("dve_router_steps")
        s_rt = sem("router_logits_less_max")
        s_exr = sem("router_exp_ready")
        s_cw = sem("chunk_weights_ready")
        s_xc = [sem(f"xn_chunk{i}_loaded") for i in range(2)]
        s_l1 = sem("hidden_done")
        s_act = [sem(f"activation{c}_ready") for c in range(FC)]
        s_l2 = [sem(f"expert_out{i}_done") for i in range(2)]
        s_comb = [sem(f"expert_out{i}_added") for i in range(2)]
        c_m = sem("dve_combine_steps")
        s_cwt = sem("chunk_weights_turned")
        s_cwe = sem("chunk_weights_turned_read")
        s_b2 = sem("bias2_done")
        s_b2a = sem("bias2_added")
        s_out = sem("out_stored")

        block = ctx.enter_context(nc.Block())

        CHUNKS = TILES // 4
        WA_LOADS = 4 + 4 + 9 + 3
        WM_LOADS = 7

        def run_turns(eng, body):
            for b in (-3, -2, -1, 0, 1):
                body(b, b % 2)
            with eng.Fori(1, 6) as g:
                for par in range(2):
                    body(g * 2 + par, par)
            for b in (12, 13, 14, 15, 16):
                body(b, b % 2)

        def run_chunks(eng, body):
            body(0)
            with eng.Fori(1, CHUNKS // 2) as g:
                body(g)

        def stored_before(b, par):
            return 8 * (b - par)

        def scores_of(b, s):
            return (b, s - SHIFT) if s >= SHIFT else (b - 1, s - SHIFT + H)

        def values_of(b, s):
            return (b, s - SHIFT - PV_LAG) if s >= SHIFT + PV_LAG else (b - 1, s - SHIFT - PV_LAG + H)

        @block.sync
        def _(sp):
            sp.dma_start(xres[:, 0:XL, :], x_d[:, 0:XL, :]).then_inc(s_x[0], 16)
            sp.dma_start(raw_sm[:, 0:RKV], W_kv).then_inc(s_wa, 16)
            sp.dma_start(raw_sm[:, RKV:RKV + RQ], W_q).then_inc(s_wa, 16)
            sp.dma_start(raw_sm[:, RKV + RQ:SMW], Wg).then_inc(s_wa, 16)
            sp.dma_start(raw_kr, W_krope).then_inc(s_wa, 16)
            for n in range(2):
                sp.dma_start(raw_qr[n * RQ:(n + 1) * RQ, :], W_qrope).then_inc(s_wa, 16)
                sp.dma_start(raw_qd[n * RQ:(n + 1) * RQ, :], W_qdec).then_inc(s_wa, 16)
            for n in range(3):
                rows = slice(n * RKV, (n + 1) * RKV)
                sp.dma_start(raw_kv[rows, 0:HD], W_kdec).then_inc(s_wa, 16)
                sp.dma_start(raw_kv[rows, HD:2 * HD], W_vdec).then_inc(s_wa, 16)
                sp.dma_start(g_rep[rows, :], g_kv.rearrange("(r a) -> r a", a=1)).then_inc(s_wa, 16)
            sp.dma_start(wo[:, :], W_o).then_inc(s_wa, 16)
            rope_v = rope.rearrange("(j p) c -> p j c", p=P)
            sp.dma_start(cosx[:, :, :], rope_v[:, :, 0:D]).then_inc(s_wa, 16)
            sp.dma_start(sins[:, :, :], rope_v[:, :, D:D + DR]).then_inc(s_wa, 16)
            for n in range(1, N_X):
                sp.dma_start(xres[:, n * XL:(n + 1) * XL, :], x_d[:, n * XL:(n + 1) * XL, :]).then_inc(s_x[n], 16)
            sp.dma_start(braw[0:E * FC, :], b1.rearrange("e (c p) -> (e c) p", p=P)).then_inc(s_wm, 16)
            sp.dma_start(braw[E * FC:NE * FC, :], bs1.rearrange("(c p) -> c p", p=P)).then_inc(s_wm, 16)
            sp.dma_start(w1raw[:, 0:E, :], W1.rearrange("e h f -> h e f")).then_inc(s_wm, 16)
            sp.dma_start(w2[:, 0:E, :, :], W2.rearrange("e (c p) h -> p e c h", p=P)).then_inc(s_wm, 16)
            sp.dma_start(w2[:, E, :, :], Ws2.rearrange("(c p) h -> p c h", p=P)).then_inc(s_wm, 16)
            sp.dma_start(b2x[0:E, :], b2).then_inc(s_wm, 16)
            sp.dma_start(b2x[E:NE, :], bs2.rearrange("(a h) -> a h", a=1)).then_inc(s_wm, 16)

            def turn(b, par):
                if known(b):
                    sp.wait_ge(s_mT, b + 1)
                    sp.dma_start(QK[KQ:KK, par, 0, :, :].bitcast(F32), mT[:, :].bitcast(F32)).then_inc(s_mrow, 16)
                if known(b + 3):
                    at = slice((b + 3) * T, (b + 4) * T) if isinstance(b, int) else bass.ds(sp.snap((b + 3) * T), T)
                    sp.wait_ge(s_xh, b + 4)
                    sp.wait_ge(s_xl, b + 4)
                    sp.wait_ge(s_x[0], 16)
                    sp.dma_start(parts_d[:, :, at].bitcast(F32), xhl[:, (par + 1) % 2, :, :].bitcast(F32)).then_inc(s_xst[(par + 1) % 2], 16)

            run_turns(sp, turn)

            sp.wait_ge(s_acc, B)
            sp.dma_start(ws1raw, Ws1).then_inc(s_ws, 16)
            for i in range(2):
                sp.wait_ge(s_xst[i], 8 * B)
            sp.wait_ge(s_bfill, B * B_UNITS)

            def load_chunk(n, at):
                sp.dma_start(xc[n].bitcast(F32), parts_d[:, :, at].bitcast(F32)).then_inc(s_xc[n], 16)

            def store_chunk(g, n):
                m = (n + 1) * NE - 1
                at = slice((2 * g + n) * 4, (2 * g + n + 1) * 4) if isinstance(g, int) else \
                    bass.ds(sp.snap(g * 8 + 4 * n), 4)
                sp.wait_ge(s_comb[m % 2], g * NE + m // 2 + 1)
                sp.wait_ge(s_x[0], 16)
                sp.dma_start(out_d[:, at, :], xres[:, at, :]).then_inc(s_out, 16)

            for n in range(2):
                load_chunk(n, slice(n * 4 * P, (n + 1) * 4 * P))
            with sp.Fori(0, CHUNKS // 2 - 1) as g:
                for n in range(2):
                    store_chunk(g, n)
                    at = bass.ds(sp.snap((g * 2 + n + 2) * (4 * P)), 4 * P)
                    sp.wait_ge(s_l1, (g * 2 + n + 1) * (NE * FC))
                    sp.wait_ge(s_x[0], 16)
                    load_chunk(n, at)
            for n in range(2):
                store_chunk(CHUNKS // 2 - 1, n)
            sp.wait_ge(s_out, 16 * CHUNKS)

        @block.gpsimd
        def _(pool):
            nc.gpsimd.memset(ident[:, :], 0.0).then_inc(s_const, 1)
            nc.gpsimd.memset(mask_qk[:, :], 0.0).then_inc(s_const, 1)
            nc.gpsimd.memset(mask_kq[:, :], 0.0).then_inc(s_const, 1)
            nc.gpsimd.memset(tri8[:, :, :], 1.0).then_inc(s_const, 1)
            pool.wait_ge(s_const, 4)
            nc.gpsimd.affine_select(out=ident[:, :], in_=ident[:, :], compare_op=ALU.not_equal, fill=1.0,
                                    base=0, pattern=[[-1, P]], channel_multiplier=1).then_inc(s_const, 1)
            nc.gpsimd.affine_select(out=mask_qk[:, :], in_=mask_qk[:, :], compare_op=ALU.is_ge, fill=NEG,
                                    base=0, pattern=[[-1, P]], channel_multiplier=1).then_inc(s_const, 1)
            nc.gpsimd.affine_select(out=mask_kq[:, :], in_=mask_kq[:, :], compare_op=ALU.is_ge, fill=NEG,
                                    base=0, pattern=[[1, P]], channel_multiplier=-1).then_inc(s_const, 1)
            nc.gpsimd.affine_select(out=tri8[:, :, :], in_=tri8[:, :, :], compare_op=ALU.is_gt, fill=0.0,
                                    base=0, pattern=[[1, E], [-1, E]], channel_multiplier=0).then_inc(s_const, 1)
            nc.gpsimd.memset(vpad[:, :], 0.0).then_inc(s_init, 1)
            pool.wait_ge(s_init, 1)
            for n in range(NT * 2):
                ones = diagonal(n * GH * P + GW)
                nc.gpsimd.memset(ones, 1.0).then_inc(s_init, 1)
            for j in range(NT):
                nc.gpsimd.memset(stk["k", j][:, :, KQ:KK].bitcast(F32), 1.0).then_inc(s_init, 1)
            nc.gpsimd.memset(wsm[:, :].bitcast(F32), 0.0).then_inc(s_init, 1)
            nc.gpsimd.memset(wqb[:, :, :].bitcast(F32), 0.0).then_inc(s_init, 1)
            nc.gpsimd.memset(cw[:, :, E:NE], 0.1).then_inc(s_init, 1)
            nc.gpsimd.memset(mhalf[:, :], -0.5).then_inc(s_init, 1)
            nc.gpsimd.memset(unit[:, :], 1.0).then_inc(s_init, 1)
            pool.wait_ge(s_init, INIT)

            def place(b, g, par):
                if g == 0:
                    pool.wait_ge(s_v, NT * (b + 1))
                at_least(pool, s_pv, (b - 1) * H + (g + 1) * GH)
                for j in range(NT):
                    nc.gpsimd.tensor_tensor(
                        diagonal((j * H + g * GH) * P),
                        vraw[:, par, j, g * GW:(g + 1) * GW].rearrange("p (h d) -> p h d", d=DC),
                        unit[:, 0:GH].unsqueeze(2).to_broadcast([P, GH, DC]), ALU.mult).then_inc(s_vp, 1)

            def stack(b, side, j):
                st = stk[side, j]
                again, low = (1, 2) if side == "q" else (2, 1)
                pool.wait_ge(s_hi[side], b * NT + j + 1)
                nc.gpsimd.tensor_tensor(st[:, :, low * D:(low + 1) * D], r[side][:, :, :], st[:, :, 0:D],
                                        ALU.subtract).then_inc(s_lo[side], 1)
                nc.gpsimd.tensor_tensor(st[:, :, again * D:(again + 1) * D], st[:, :, 0:D],
                                        unit[:, :].unsqueeze(2).to_broadcast([P, H, D]), ALU.mult).then_inc(s_dup[side], 1)

            def turn(b, par):
                for s in range(STEPS):
                    if known(b) and s == 0:
                        place(b, 0, par)
                    if known(b) and s == SHIFT + PV_LAG - 1:
                        place(b, 1, par)
                    if known(b + 2) and s in HIGH_AT:
                        stack(b + 2, *HIGH_AT[s])
                    if known(b + 3) and s == XT_STEP - 2:
                        pool.wait_ge(s_var, b + 4)
                        nc.gpsimd.tensor_tensor(rstd[:, :], rstd[:, :], mhalf[:, :], ALU.pow).then_inc(s_rstd, 1)
                    if known(b + 3) and s == SM_STEP + 1:
                        pool.wait_ge(s_ms, b + 4)
                        nc.gpsimd.tensor_tensor(rs[:, :], rs[:, :], mhalf[:, :], ALU.pow).then_inc(s_rs, 1)

            run_turns(pool, turn)

        @block.scalar
        def _(sc):
            act_f = nc.scalar.activation
            sc.wait_ge(s_const, 8)
            act_f(identr[:, :], ident[:, :], ACT.Copy).then_inc(s_cast, 1)
            act_f(identb[:, :], ident[:, :], ACT.Copy).then_inc(s_cast, 1)
            sc.wait_ge(s_biasT, 1)
            act_f(bias1[:, :], banks[1][:, 0:NE * FC], ACT.Copy).then_inc(s_bias, 1)

            def turn(b, par):
                for s in range(STEPS):
                    bb, h = scores_of(b, s)
                    if known(bb):
                        n = bb * H + h
                        sc.wait_ge(s_st, n + 1)
                        at_least(sc, s_pv, n - 3)
                        act_f(prob[:, h % 4, :], ST_PS[h % 2][:, 0:3 * P], ACT.Exp, scale=SCALE).then_inc(s_exp, 1)
                    bb, h = values_of(b, s)
                    if known(bb) and h % GH == GH - 1:
                        g = h // GH
                        rows = slice(g * GW, (g + 1) * GW)
                        sc.wait_ge(s_pv, bb * H + h + 1)
                        at_least(sc, s_oT, bb)
                        act_f(num[rows], PV_PS[g][0:GW, 0:T], ACT.Copy).then_inc(s_ev, 1)
                        act_f(den[rows], PV_PS[g][GW:2 * GW, 0:T], ACT.Copy).then_inc(s_ev, 1)
                    if s == MT_STEP and known(b):
                        sc.wait_ge(s_bfill, (b + 1) * B_UNITS)
                        at_least(sc, s_mrow, 16 * b)
                        act_f(mT[:, :], B_PS[0][0:2 * H, 0:T], ACT.Copy).then_inc(s_mT, 1)
                    if known(b + 1):
                        for what in UNITS_AT.get(s, ()):
                            if what[0] == "s" or by_dve(what):
                                continue
                            _, j, side, h0 = what
                            rows = KK if side == "k" else KQ
                            bank = bank_of(what)
                            sc.wait_ge(s_bfill, (b + 1) * B_UNITS + units_until(what))
                            at_least(sc, s_st, (b - 1) * H + h0 + 4)
                            act_f(QK[0:rows, (par + 1) % 2, "qk".index(side), h0:h0 + 4, j * P:(j + 1) * P],
                                  B_PS[bank][0:rows, :].rearrange("p (h t) -> p h t", h=4),
                                  ACT.Copy).then_inc(s_bfree[bank], 1)
                    if known(b + 2) and s in ROT_AT:
                        side, j = ROT_AT[s]
                        n = (b + 2) * NT + j
                        if side == "k":
                            sc.wait_ge(s_pfill, (b + 2) * PROJ_UNITS + 2 * order_of(side, j) + 1)
                            at_least(sc, s_vp, 2 * NT * (b + 1))
                            act_f(vraw[:, par, j, :], banks[0][:, HD:2 * HD], ACT.Copy).then_inc(s_v, 1)
                            at_least(sc, s_lo["k"], n)
                            act_f(r["k"][:, :, 0:DC], banks[0][:, 0:HD].rearrange("p (h d) -> p h d", h=H),
                                  ACT.Copy).then_inc(s_pfree[0], 1)
                    if known(b + 2) and s in HIGH_AT:
                        side, j = HIGH_AT[s]
                        n = (b + 2) * NT + j
                        if side == "k":
                            sc.wait_ge(s_pfree[0], (b + 2) * 4 + order_of(side, j) + 1)
                        sc.wait_ge(s_rot[side], n + 1)
                        at_least(sc, s_bfill, (b + 1) * B_UNITS + units_until(("t", j, side, H - 4)) if known(b + 1) else 0)
                        act_f(stk[side, j][:, :, 0:D], r[side][:, :, :], ACT.Copy).then_inc(s_hi[side], 1)
                    if known(b + 3) and s == XT_STEP:
                        sc.wait_ge(s_afill, (b + 3) * 3 + 1)
                        at_least(sc, s_xst[(par + 1) % 2], stored_before(b + 3, (par + 1) % 2))
                        at_least(sc, s_pfill, (b + 2) * PROJ_UNITS)
                        act_f(xhl[:, (par + 1) % 2, 0, :], banks[0][:, 0:T], ACT.Copy).then_inc(s_xh, 1)
                    if known(b + 3) and s == SM_STEP:
                        sc.wait_ge(s_afill, (b + 3) * 3 + 2)
                        at_least(sc, s_small, b + 3)
                        act_f(smt[:, :, :], banks[1][:, :].rearrange("p (j c) -> p j c", j=NT)[:, :, 0:SMW],
                              ACT.Copy).then_inc(s_smh, 1)
                    if known(b + 3) and s == QK_STEP:
                        sc.wait_ge(s_afill, (b + 3) * 3 + 3)
                        at_least(sc, s_pfill, (b + 3) * PROJ_UNITS)
                        act_f(qsT[:, :, :], banks[0][:, 0:T].rearrange("p (j t) -> p j t", j=NT),
                              ACT.Copy).then_inc(s_smT, 1)
                        act_f(ksT[:, :, :], banks[0][0:3 * RKV, T:2 * T].rearrange("p (j t) -> p j t", j=NT),
                              ACT.Copy).then_inc(s_smT, 1)
                    if isinstance(b, int) and b == B - 1:
                        if s == 2:
                            sc.wait_ge(s_rt, 1)
                            act_f(pr, pr, ACT.Exp).then_inc(s_exr, 1)
                        if 5 <= s < 5 + E:
                            e = s - 5
                            if e == 0:
                                sc.wait_ge(s_wm, 16 * WM_LOADS)
                                sc.wait_ge(s_st, (B - 1) * H)
                            act_f(w1_part(e, 0, 0, F), w1raw[:, e, :], ACT.Copy).then_inc(s_w1h, 1)

            run_turns(sc, turn)

            sc.wait_ge(s_ws, 16)
            act_f(w1_part(E, 0, 0, F), ws1raw, ACT.Copy).then_inc(s_w1h, 1)

            def chunks(g):
                for n in range(2):
                    sc.wait_ge(s_cwt, g * 2 + n + 1)
                    act_f(cwT[:, :], banks[7][0:NE, :], ACT.Copy).then_inc(s_cwe, 1)
                    for e in range(NE):
                        m = n * NE + e
                        for c in range(FC):
                            k = e * FC + c
                            sc.wait_ge(s_l1, g * (2 * NE * FC) + m * FC + c + 1)
                            if c == 0:
                                at_least(sc, s_l2[m % 2], g * NE + m // 2)
                            act_f(act[:, m % 2, c, :], banks[c][:, :], ACT.Silu,
                                  bias=bias1[:, k:k + 1]).then_inc(s_act[c], 1)

            run_chunks(sc, chunks)

        @block.vector
        def _(dve):
            V = nc.vector

            steps = Chain(dve, c_s, 0, 0)
            dve.wait_ge(s_wa, 16 * WA_LOADS)
            dve.wait_ge(s_init, INIT)
            steps.add(V.tensor_scalar(raw_kv, raw_kv, g_rep, None, ALU.mult))
            steps.add(V.tensor_copy(wsm[:, 0:SMW], raw_sm))
            steps.add(V.tensor_copy(wkr[:, 0, :], raw_kr))
            steps.add(V.tensor_copy(wqa[:, :, 0:DC], raw_qd.rearrange("p (h d) -> p h d", h=H)))
            steps.add(V.tensor_copy(wqa[:, :, DC:D], raw_qr.rearrange("p (h d) -> p h d", h=H)))
            steps.need()
            steps.add(V.tensor_copy(kv_hi, raw_kv))
            steps.add(V.tensor_tensor(wsm[:, P:P + SMW], raw_sm, wsm[:, 0:SMW], ALU.subtract))
            steps.add(V.tensor_tensor(wkr[:, 1, :], raw_kr, wkr[:, 0, :], ALU.subtract))
            steps.add(V.tensor_tensor(wqb[0:RQ, :, 0:DC], raw_qd[0:RQ, :].rearrange("p (h d) -> p h d", h=H),
                                      wqa[0:RQ, :, 0:DC], ALU.subtract))
            steps.add(V.tensor_tensor(wqb[0:RQ, :, DC:D], raw_qr[0:RQ, :].rearrange("p (h d) -> p h d", h=H),
                                      wqa[0:RQ, :, DC:D], ALU.subtract))
            steps.need()
            steps.add(V.tensor_copy(wkv[0:2 * RKV, :], raw_kv[0:2 * RKV, :]))
            steps.need()
            V.tensor_tensor(wkv[2 * RKV:3 * RKV, :], raw_kv[2 * RKV:3 * RKV, :], kv_hi[2 * RKV:3 * RKV, :],
                            ALU.subtract).then_inc(s_wsplit, 1)
            dve.wait_ge(s_wsplit, 1)

            def normalise(b, steps):
                i = b * NT
                at_least(dve, c_a, b * SMALL_STEPS)
                at_least(dve, s_xn, b * NT)
                for n in range(N_X):
                    if not isinstance(b, int) or n == i // XL:
                        dve.wait_ge(s_x[n], 16)
                for j in range(NT):
                    at = slice(i + j, i + j + 1) if isinstance(b, int) else bass.ds(i + j, 1)
                    steps.add(V.bn_stats(st6[:, j, :], xres[:, at, :]))
                steps.need()
                steps.add(V.memset(pace[:, :], 0.0))
                for j in range(NT):
                    steps.add(V.bn_aggr(mv[:, j, :], st6[:, j, :]))
                steps.need()
                V.tensor_scalar(rstd[:, :], mv[:, :, 1], LN_EPS, None, ALU.add).then_inc(s_var, 1)

            def normalised(b):
                i = b * NT
                dve.wait_ge(s_rstd, b + 1)
                at_least(dve, s_afill, 3 * b - 2)
                for j in range(NT):
                    at = slice(i + j, i + j + 1) if isinstance(b, int) else bass.ds(i + j, 1)
                    V.tensor_scalar(xn[:, j:j + 1, :], xres[:, at, :], mv[:, j, 0:1], rstd[:, j:j + 1],
                                    ALU.subtract, ALU.mult).then_inc(s_xn, 1)

            def small_products(b, steps):
                low = banks[1][:, :].rearrange("p (j c) -> p j c", j=NT)
                dve.wait_ge(s_smh, b + 1)
                at = slice(b * NT, (b + 1) * NT) if isinstance(b, int) else bass.ds(b * NT, NT)
                steps.add(V.tensor_tensor(lg[:, at, :], low[:, :, P + RKV + RQ:P + SMW], smt[:, :, RKV + RQ:SMW], ALU.add))
                steps.add(V.tensor_tensor(smt[:, :, 0:RKV + RQ], low[:, :, P:P + RKV + RQ],
                                          smt[:, :, 0:RKV + RQ], ALU.add))
                steps.need()
                kv, qc = smt[:, :, 0:RKV], smt[:, :, RKV:RKV + RQ]
                steps.add(V.tensor_tensor(sq[:, :, :], kv, kv, ALU.mult))
                at_least(dve, s_afill, 3 * b)
                steps.add(V.tensor_copy(qs[:, :, 0, :], qc))
                steps.need()
                steps.add(V.tensor_reduce(ss[:, :], sq[:, :, :], AX.X, ALU.add))
                steps.need()
                V.tensor_scalar(rs[:, :], ss[:, :], 1.0 / RKV, RMS_EPS, ALU.mult, ALU.add).then_inc(s_ms, 1)

            def small_stacks(b, steps):
                kv, qc = smt[:, :, 0:RKV], smt[:, :, RKV:RKV + RQ]
                dve.wait_ge(s_rs, b + 1)
                steps.add(V.tensor_tensor(kv, kv, rs[:, :].unsqueeze(2).to_broadcast([P, NT, RKV]), ALU.mult))
                steps.need()
                steps.add(V.tensor_copy(ks[:, :, 0:3:2, :], kv.unsqueeze(2).to_broadcast([P, NT, 2, RKV])))
                steps.need()
                steps.add(V.tensor_tensor(ks[:, :, 1, :], kv, ks[:, :, 0, :], ALU.subtract))
                V.tensor_tensor(qs[:, :, 1, :], qc, qs[:, :, 0, :], ALU.subtract).then_inc(s_small, 1)

            def rotate(b, side, j, steps):
                n = b * NT + j
                out = r[side]
                at_least(dve, s_hi[side], n)
                at_least(dve, s_lo[side], n)
                order = order_of(side, j)
                for other in "qk":
                    at_least(dve, s_rot[other], b * NT + sum(order_of(other, i) < order for i in range(NT)))
                if side == "q":
                    for half in range(2):
                        hs = slice(half * GH, (half + 1) * GH)
                        bank = 1 - half
                        dve.wait_ge(s_pfill, b * PROJ_UNITS + 2 * order + half + 1)
                        ps = banks[bank][:, 0:GH * D].rearrange("p (h d) -> p h d", h=GH)
                        steps.add(V.tensor_tensor(out[:, hs, :], ps,
                                                  cosx[:, j, :].unsqueeze(1).to_broadcast([P, GH, D]), ALU.mult))
                        turned(ps[:, :, DC:D], hs, j, steps, bank)
                else:
                    dve.wait_ge(s_pfill, b * PROJ_UNITS + 2 * order + 2)
                    ps = banks[1][:, :].rearrange("p (h d) -> p h d", h=H)
                    steps.add(V.tensor_tensor(out[:, :, DC:D], ps,
                                              cosx[:, j, DC:D].unsqueeze(1).to_broadcast([P, H, DR]), ALU.mult))
                    turned(ps, slice(0, H), j, steps, 1)
                steps.need()
                dve.wait_ge(s_pfree[1], b * 4 + order + 1)
                if side == "q":
                    dve.wait_ge(s_pfree[0], b * 4 + order + 1)
                V.tensor_tensor(out[:, :, DC:D], out[:, :, DC:D], t2[:, :, :], ALU.add).then_inc(s_rot[side], 1)

            def turned(ps, hs, j, steps, bank):
                hh, n = DR // 2, hs.stop - hs.start
                steps.add(V.tensor_tensor(t2[:, hs, 0:hh], ps[:, :, hh:DR],
                                          sins[:, j, 0:hh].unsqueeze(1).to_broadcast([P, n, hh]), ALU.mult))
                V.tensor_tensor(t2[:, hs, hh:DR], ps[:, :, 0:hh],
                                sins[:, j, hh:DR].unsqueeze(1).to_broadcast([P, n, hh]), ALU.mult)\
                    .then_inc(s_pfree[bank], 1)

            def place_stack(b, what, par):
                _, j, side, h0 = what
                rows = KK if side == "k" else KQ
                bank = bank_of(what)
                dve.wait_ge(s_bfill, b * B_UNITS + units_until(what))
                at_least(dve, s_st, (b - 2) * H + h0 + 4)
                V.tensor_copy(QK[0:rows, par, "qk".index(side), h0:h0 + 4, j * P:(j + 1) * P],
                              B_PS[bank][0:rows, :].rearrange("p (h t) -> p h t", h=4)).then_inc(s_bfree[bank], 1)

            def router():
                steps = Chain(dve, c_rt, 0, 0)
                bc = lambda t: t.unsqueeze(2).to_broadcast([P, TILES, E])
                top, tot, inv = rsm[:, 0, :], rsm[:, 1, :], rsm[:, 2, :]
                dve.wait_ge(c_a, B * SMALL_STEPS)
                for side in "qk":
                    dve.wait_ge(s_rot[side], TILES)
                    dve.wait_ge(s_hi[side], TILES)
                    dve.wait_ge(s_lo[side], TILES)
                steps.add(V.tensor_reduce(top, lg[:, :, :], AX.X, ALU.max))
                steps.need()
                V.tensor_tensor(pr, lg[:, :, :], bc(top), ALU.subtract).then_inc(s_rt, 1)
                dve.wait_ge(s_exr, 1)
                steps.add(V.tensor_reduce(tot, pr, AX.X, ALU.add))
                steps.need()
                steps.add(V.reciprocal(inv, tot))
                steps.need()
                steps.add(V.tensor_tensor(pr, pr, bc(inv), ALU.mult))
                steps.need()
                for q in range(TILES // 8):
                    ts = slice(8 * q, 8 * q + 8)
                    mine = pr[:, ts, :].unsqueeze(3).to_broadcast([P, 8, E, E])
                    other = pr[:, ts, :].unsqueeze(2).to_broadcast([P, 8, E, E])
                    steps.add(V.tensor_tensor(cmp_gt, other, mine, ALU.is_gt))
                    steps.add(V.tensor_tensor(cmp_eq, other, mine, ALU.is_equal))
                    steps.need()
                    steps.add(V.tensor_tensor(cmp_eq, cmp_eq, tri8[:, :, :].unsqueeze(1).to_broadcast([P, 8, E, E]), ALU.mult))
                    steps.need()
                    steps.add(V.tensor_tensor(cmp_gt, cmp_gt, cmp_eq, ALU.add))
                    steps.need()
                    steps.add(V.tensor_reduce(rank[:, ts, :], cmp_gt, AX.X, ALU.add))
                    steps.need()
                steps.add(V.tensor_scalar(rank, rank, 2.0, None, ALU.is_lt))
                steps.need()
                steps.add(V.tensor_tensor(pr, pr, rank, ALU.mult))
                steps.need()
                steps.add(V.tensor_reduce(tot, pr, AX.X, ALU.add))
                steps.need()
                steps.add(V.tensor_scalar(tot, tot, TOP_EPS, None, ALU.add))
                steps.need()
                steps.add(V.reciprocal(inv, tot))
                steps.need()
                steps.add(V.tensor_tensor(cw[:, :, 0:E], pr, bc(inv), ALU.mult))
                steps.need()

            def turn(b, par):
                small = Chain(dve, c_a, b + 3, SMALL_STEPS)
                rot = Chain(dve, c_r, b + 2, ROT_STEPS)
                for s in range(STEPS):
                    if known(b - 1) and s == SHIFT + PV_LAG + 1:
                        dve.wait_ge(s_ev, 4 * b)
                        V.reciprocal(den, den).then_inc(c_c, 1)
                        dve.wait_ge(c_c, b)
                        at_least(dve, s_wo, b - 1)
                        V.tensor_tensor(oT[:, :], num, den, ALU.mult).then_inc(s_oT, 1)
                    if known(b - 1) and s == WO_STEP + 1:
                        dve.wait_ge(s_wo, b)
                        at = slice((b - 1) * NT, b * NT) if isinstance(b, int) else bass.ds((b - 1) * NT, NT)
                        V.tensor_tensor(xres[:, at, :], PV_PS[1][:, 0:T].rearrange("p (j c) -> p j c", j=NT),
                                        xres[:, at, :], ALU.add).then_inc(s_acc, 1)
                    if known(b + 2) and s in ROT_AT:
                        rotate(b + 2, *ROT_AT[s], rot)
                    if known(b + 1):
                        for what in UNITS_AT.get(s, ()):
                            if by_dve(what):
                                place_stack(b + 1, what, (par + 1) % 2)
                        for what in UNITS_AT.get(s, ()):
                            if what[0] == "t":
                                continue
                            h, bank = what[1], bank_of(what)
                            dve.wait_ge(s_bfill, (b + 1) * B_UNITS + units_until(what))
                            ps = B_PS[bank]
                            V.tensor_reduce(mx[:, 0, h:h + 1], ps[:, 0:P], AX.X, ALU.max).then_inc(c_b, 1)
                            V.tensor_reduce(mx[:, 1, h:h + 1], ps[:, T:2 * T], AX.X, ALU.max).then_inc(s_bfree[bank], 1)
                        if s == max(UNITS_AT):
                            dve.wait_ge(c_b, (b + 2) * H)
                            for i in range(2):
                                dve.wait_ge(s_bfree[i], (b + 2) * B_FREES)
                            at_least(dve, s_bfill, (b + 1) * B_UNITS)
                            V.tensor_scalar(nhl[:, :, 0, :], mx[:, :, :], -1.0, None, ALU.mult).then_inc(c_n, 1)
                            dve.wait_ge(c_n, b + 2)
                            V.scalar_tensor_tensor(out=nhl[:, :, 1, :], in0=mx[:, :, :], scalar=-1.0,
                                                   in1=nhl[:, :, 0, :], op0=ALU.mult, op1=ALU.subtract).then_inc(s_nm, 1)
                    if known(b + 3):
                        if s == XT_STEP - 3:
                            normalise(b + 3, small)
                        if s == XT_STEP - 1:
                            normalised(b + 3)
                        if s == XT_STEP + 1:
                            dve.wait_ge(s_xh, b + 4)
                            V.tensor_tensor(xhl[:, (par + 1) % 2, 1, :], banks[0][:, 0:T], xhl[:, (par + 1) % 2, 0, :],
                                            ALU.subtract).then_inc(s_xl, 1)
                        if s == SM_STEP:
                            small_products(b + 3, small)
                        if s == SM_STEP + 2:
                            small_stacks(b + 3, small)
                    if isinstance(b, int) and b == B - 1:
                        if s == 0:
                            router()
                        if 5 <= s < 5 + E:
                            e = s - 5
                            dve.wait_ge(s_w1h, e + 1)
                            V.tensor_tensor(w1_part(e, 1, 0, F), w1raw[:, e, :], w1_part(e, 0, 0, F),
                                            ALU.subtract).then_inc(s_w1l, 1)
                assert not known(b + 3) or small.n == SMALL_STEPS, small.n
                assert not known(b + 2) or rot.n == ROT_STEPS, rot.n

            run_turns(dve, turn)

            dve.wait_ge(s_w1h, NE)
            V.tensor_tensor(w1_part(E, 1, 0, F), ws1raw, w1_part(E, 0, 0, F), ALU.subtract).then_inc(s_w1l, 1)
            dve.wait_ge(s_acc, B)

            def chunks(g):
                for n in range(2):
                    for i in range(2):
                        at_least(dve, s_comb[i], g * NE)
                    at_least(dve, c_m, g * (2 * NE * 3))
                    chunk = bass.ds(g * 8 + 4 * n, 4)
                    V.tensor_copy(cwc[:, n, :, :], cw[:, chunk, :]).then_inc(s_cw, 1)
                    dve.wait_ge(s_cw, g * 2 + n + 1)
                    dve.wait_ge(s_b2, g * 2 + n + 1)
                    V.tensor_tensor(xres[:, chunk, :], banks[6][:, :].rearrange("p (i c) -> p i c", i=4),
                                    xres[:, chunk, :], ALU.add).then_inc(s_b2a, 1)
                    dve.wait_ge(s_b2a, g * 2 + n + 1)
                    for e in range(NE):
                        m = n * NE + e
                        dve.wait_ge(s_l2[m % 2], g * NE + m // 2 + 1)
                        if e:
                            dve.wait_ge(c_m, (g * 2 * NE + m) * 3)
                            dve.wait_ge(s_comb[(m - 1) % 2], g * NE + (m - 1) // 2 + 1)
                        for i in range(4):
                            tile = xres[:, bass.ds(g * 8 + 4 * n + i, 1), :].squeeze(1)
                            V.scalar_tensor_tensor(out=tile, in0=banks[4 + m % 2][:, i * P:(i + 1) * P],
                                                   scalar=cwc[:, n, i, e:e + 1], in1=tile, op0=ALU.mult,
                                                   op1=ALU.add).then_inc(c_m if i < 3 else s_comb[m % 2], 1)

            run_chunks(dve, chunks)

        @block.tensor
        def _(pe):
            mm = nc.tensor.matmul
            pe.wait_ge(s_const, 8)
            pe.wait_ge(s_wm, 16 * WM_LOADS)
            nc.tensor.transpose(banks[1][:, 0:NE * FC], braw, ident[0:NE * FC, 0:NE * FC]).then_inc(s_biasT, 1)
            pe.wait_ge(s_cast, 2)
            pe.wait_ge(s_bias, 1)
            pe.wait_ge(s_wsplit, 1)

            def head_scores(b, h, par):
                ps, n = ST_PS[h % 2], b * H + h
                q, k = QK[0:KK, par, 0, h, :], QK[0:KK, par, 1, h, :]
                if h == 0:
                    pe.wait_ge(s_mrow, 16 * (b + 1))
                at_least(pe, s_exp, n - 1)
                mm(ps[:, P:3 * P], k[:, P:T], q, start=True, stop=False, skip_group_check=True)
                mm(ps[:, T:3 * P], identb[:, :], mask_kq[:, :], start=False, stop=True, skip_group_check=True)
                mm(ps[:, 0:T], k[:, 0:P], q, start=True, stop=False, skip_group_check=True)
                mm(ps[:, 0:P], identb[:, :], mask_kq[:, :], start=False, stop=True,
                   skip_group_check=True).then_inc(s_st, 1)

            def head_values(b, h):
                g, ps = h // GH, PV_PS[h // GH]
                if h % GH == 0:
                    pe.wait_ge(s_vp, (2 * b + g + 1) * NT)
                    at_least(pe, s_ev, 4 * b - 2 + 2 * g)
                    if g == 1:
                        at_least(pe, s_acc, b)
                pe.wait_ge(s_exp, b * H + h + 1)
                p = prob[:, h % 4, :]
                mm(ps[:, 0:T], vpad[:, h * P:(h + 1) * P], p[:, 0:T], start=(h % GH == 0), stop=False)
                mm(ps[:, P:T], vpad[:, (H + h) * P:(H + h + 1) * P], p[:, T:3 * P],
                   start=False, stop=(h % GH == GH - 1)).then_inc(s_pv, 1)

            def output_projection(b):
                pe.wait_ge(s_oT, b + 1)
                for j in range(NT):
                    ins = mm(PV_PS[1][:, j * P:(j + 1) * P], oT[:, j * P:(j + 1) * P], wo[:, :], start=True, stop=True)
                ins.then_inc(s_wo, 1)

            def turn_stacks(b, what):
                _, j, side, h0 = what
                rows = KK if side == "k" else KQ
                u, bank = UNITS.index(what), bank_of(what)
                if h0 == 0:
                    pe.wait_ge(s_dup[side], b * NT + j + 1)
                    pe.wait_ge(s_lo[side], b * NT + j + 1)
                at_least(pe, s_bfree[bank], b * B_FREES + u // 2)
                if u == 1:
                    at_least(pe, s_mT, b)
                for i in range(4):
                    ins = nc.tensor.transpose(B_PS[bank][0:rows, i * P:(i + 1) * P].bitcast(F32R),
                                              stk[side, j][:, h0 + i, 0:rows], identr[:, :])
                ins.then_inc(s_bfill, 1)

            def scores_for_max(b, what, par):
                h, u, bank = what[1], UNITS.index(what), bank_of(what)
                ps = B_PS[bank]
                q, k = QK[0:KQ, par, 0, h, :], QK[0:KQ, par, 1, h, :]
                last = max((("t", j, side, h // 4 * 4) for j in range(NT) for side in "qk"), key=UNITS.index)
                for i in range(2):
                    n = max(u // 2 if i == bank else 0, uses_until(last, i) if h % 4 == 0 else 0)
                    if n:
                        pe.wait_ge(s_bfree[i], b * B_FREES + n)
                mm(ps[:, 0:T], q[:, 0:P], k, start=True, stop=False, skip_group_check=True)
                mm(ps[:, T:2 * T], q[:, P:T], k, start=False, stop=False, skip_group_check=True)
                diag = ps[:, :].rearrange("p (a c) -> p a c", a=4)[:, 0:4:3, :]
                mm(diag, identb[:, :], mask_qk[:, :].unsqueeze(1).to_broadcast([P, 2, P]), start=False, stop=True,
                   skip_group_check=True).then_inc(s_bfill, 1)

            def turn_maxima(b):
                pe.wait_ge(s_nm, b + 1)
                pe.wait_ge(s_bfree[0], (b + 1) * B_FREES)
                for j in range(NT):
                    ins = nc.tensor.transpose(B_PS[0][0:2 * H, j * P:(j + 1) * P].bitcast(F32R),
                                              nhl[:, j, :, :].rearrange("p a h -> p (a h)"), identr[:, :])
                ins.then_inc(s_bfill, 1)

            def project(b, side, j, par):
                k0 = b * 4 + order_of(side, j)
                qrow, kvrow = qsT[:, j, :], ksT[:, j, :]
                xh, xl = (xhl[:, par, a, j * P:(j + 1) * P] for a in range(2))
                pe.wait_ge(s_smT, 2 * (b + 1))
                if side == "q":
                    for half in range(2):
                        bank = 1 - half
                        at_least(pe, s_pfree[bank], k0)
                        hs = slice(half * GH, (half + 1) * GH)
                        ps = banks[bank][:, 0:GH * D]
                        mm(ps, qrow, wqa[:, hs, :].rearrange("p h d -> p (h d)"), start=True, stop=False)
                        mm(ps, qrow, wqb[:, hs, :].rearrange("p h d -> p (h d)"), start=False, stop=True)\
                            .then_inc(s_pfill, 1)
                else:
                    pe.wait_ge(s_pfree[0], k0)
                    mm(banks[0][:, 0:2 * HD], kvrow, wkv[:, :], start=True, stop=True).then_inc(s_pfill, 1)
                    pe.wait_ge(s_pfree[1], k0)
                    mm(banks[1][:, :], xh, wkr[:, 0, :], start=True, stop=False)
                    mm(banks[1][:, :], xl, wkr[:, 0, :], start=False, stop=False)
                    mm(banks[1][:, :], xh, wkr[:, 1, :], start=False, stop=True).then_inc(s_pfill, 1)

            def values_and_projection(b, s):
                bb, h = values_of(b, s)
                if known(bb):
                    head_values(bb, h)
                if s == WO_STEP and known(b - 1):
                    output_projection(b - 1)

            def turn(b, par):
                for s in range(STEPS):
                    bb, h = scores_of(b, s)
                    if known(bb):
                        head_scores(bb, h, par if s >= SHIFT else (par + 1) % 2)
                    if s == MT_STEP and known(b):
                        turn_maxima(b)
                    for i, what in enumerate(UNITS_AT.get(s, ())):
                        if i == 1:
                            values_and_projection(b, s)
                        if known(b + 1):
                            if what[0] == "t":
                                turn_stacks(b + 1, what)
                            else:
                                scores_for_max(b + 1, what, (par + 1) % 2)
                    if len(UNITS_AT.get(s, ())) < 2:
                        values_and_projection(b, s)
                    if known(b + 2) and s in PROJ_AT:
                        project(b + 2, *PROJ_AT[s], par)
                    if known(b + 3):
                        if s == XT_STEP:
                            pe.wait_ge(s_xn, NT * (b + 4))
                            at_least(pe, s_pfree[0], 4 * (b + 3))
                            for j in range(NT):
                                ins = nc.tensor.transpose(banks[0][:, j * P:(j + 1) * P], xn[:, j, :], ident[:, :])
                            ins.then_inc(s_afill, 1)
                        if s == SM_STEP:
                            pe.wait_ge(s_xl, b + 4)
                            at_least(pe, s_pfree[1], 4 * (b + 3))
                            for j in range(NT):
                                for a in range(2):
                                    ins = mm(banks[1][:, j * T:(j + 1) * T],
                                             xhl[:, (par + 1) % 2, a, j * P:(j + 1) * P], wsm[:, :],
                                             start=(a == 0), stop=(a == 1))
                            ins.then_inc(s_afill, 1)
                        if s == QK_STEP:
                            pe.wait_ge(s_small, b + 4)
                            for j in range(NT):
                                nc.tensor.transpose(banks[0][:, j * P:(j + 1) * P].bitcast(F32R),
                                                    qs[:, j, :, :].rearrange("p a r -> p (a r)"), identr[:, :])
                            for j in range(NT):
                                ins = nc.tensor.transpose(banks[0][0:3 * RKV, (NT + j) * P:(NT + j + 1) * P].bitcast(F32R),
                                                          ks[:, j, :, :].rearrange("p a r -> p (a r)"), identr[:, :])
                            ins.then_inc(s_afill, 1)

            run_turns(pe, turn)

            for i in range(2):
                pe.wait_ge(s_pfree[i], 4 * B)
                pe.wait_ge(s_bfree[i], B_FREES * B)
            pe.wait_ge(s_exp, H * B)
            pe.wait_ge(s_ev, 4 * B)
            pe.wait_ge(s_acc, B)

            def hidden(g, n, e):
                m = n * NE + e
                if n == 0 and e in (0, E):
                    pe.wait_ge(s_w1l, E if e == 0 else NE)
                if e == 0:
                    pe.wait_ge(s_xc[n], (g + 1) * 16)
                for c in range(FC):
                    at_least(pe, s_act[c], g * (2 * NE) + m)
                    for i, (w, a) in enumerate(((0, 0), (0, 1), (1, 0))):
                        ins = mm(banks[c][:, :], w1_part(e, w, c * P, P), xc[n][:, a, :], start=(i == 0), stop=(i == 2))
                    ins.then_inc(s_l1, 1)

            def expert_out(g, n, e):
                m = n * NE + e
                pe.wait_ge(s_act[FC - 1], g * (2 * NE) + m + 1)
                at_least(pe, s_comb[m % 2], g * NE + m // 2)
                for i in range(4):
                    for c in range(FC):
                        ins = mm(banks[4 + m % 2][:, i * P:(i + 1) * P], act[:, m % 2, c, i * P:(i + 1) * P],
                                 w2[:, e, c, :], start=(c == 0), stop=(c == FC - 1))
                ins.then_inc(s_l2[m % 2], 1)

            def chunks(g):
                for n in range(2):
                    hidden(g, n, 0)
                    pe.wait_ge(s_cw, g * 2 + n + 1)
                    for i in range(4):
                        ins = nc.tensor.transpose(banks[7][0:NE, i * P:(i + 1) * P], cwc[:, n, i, :], ident[:, :])
                    ins.then_inc(s_cwt, 1)
                    hidden(g, n, 1)
                    pe.wait_ge(s_cwe, g * 2 + n + 1)
                    at_least(pe, s_b2a, g * 2 + n)
                    for i in range(4):
                        ins = mm(banks[6][:, i * P:(i + 1) * P], cwT[:, i * P:(i + 1) * P], b2x[:, :], start=True, stop=True)
                    ins.then_inc(s_b2, 1)
                    for e in range(NE):
                        if 2 <= e + 1 < NE:
                            hidden(g, n, e + 1)
                        expert_out(g, n, e)

            run_chunks(pe, chunks)


_INS = ['L0_attn_x', 'L0_attn_W_kv', 'L0_attn_g_kv', 'L0_attn_W_kdec', 'L0_attn_W_vdec', 'L0_attn_W_q',
        'L0_attn_W_qdec', 'L0_attn_W_krope', 'L0_attn_W_qrope', 'L0_attn_W_o', 'L0_ffn_Wg', 'L0_ffn_W1',
        'L0_ffn_b1', 'L0_ffn_W2', 'L0_ffn_b2', 'L0_ffn_Ws1', 'L0_ffn_bs1', 'L0_ffn_Ws2', 'L0_ffn_bs2']


def rope_table(np):
    inv_freq = 1.0 / 10000.0 ** (np.arange(0, DR, 2, dtype=np.float32) / DR)
    freqs = np.outer(np.arange(T, dtype=np.float32), inv_freq)
    cos, sin = np.cos(freqs), np.sin(freqs)
    return np.concatenate([np.ones((T, DC)), cos, cos, -sin, sin], -1).astype(np.float32)


def kernel(**inputs):
    import numpy as np
    import concourse.bacc as bacc
    from concourse.bass_utils import run_bass_kernel_spmd

    nc = bacc.Bacc("TRN2", target_bir_lowering=False, num_devices=1)
    arrays, args = {}, []
    for name in _INS:
        a = np.ascontiguousarray(inputs[name])
        arrays[f"in_{name}"] = a
        args.append(nc.dram_tensor(f"in_{name}", a.shape, mybir.dt.from_np(a.dtype), kind="ExternalInput").ap())
    table = rope_table(np)
    arrays["in_rope"] = table
    args.append(nc.dram_tensor("in_rope", table.shape, F32, kind="ExternalInput").ap())
    args.append(nc.dram_tensor("out", (B, T, C), F32, kind="ExternalOutput").ap())
    build(nc, *args)
    r = run_bass_kernel_spmd(nc, [arrays], core_ids=[0])
    return r.results[0]["out"]
```

```python
from contextlib import ExitStack

import concourse.bass as bass
from concourse import mybir

F32 = mybir.dt.float32
F32R = mybir.dt.float32r
BF16 = mybir.dt.bfloat16
ALU = mybir.AluOpType
ACT = mybir.ActivationFunctionType
AX = mybir.AxisListType

P = 128
B, T, C = 16, 256, 128
NT = T // P
TILES = B * NT
H, DC, DR = 16, 8, 32
D = DC + DR
HD = H * DC
RKV, RQ = 32, 64
E, F = 8, 512
FC = F // P
NE = E + 1
SCALE = float(D) ** -0.5
NEG = -1.0e30
KQ = 3 * D
KK = KQ + 2
GH = H // 2
GW = GH * DC
SMW = RKV + RQ + E
DIAG = P + DC
LN_EPS, RMS_EPS, TOP_EPS = 1e-5, 1e-6, 1e-9
SMALL_STEPS, ROT_STEPS = 13, 2 * (4 + 2)
INIT = 1 + NT * 2 + NT + 5

STEPS = H
SHIFT = 3
PV_LAG = 2
UNITS_AT = {
    1: (("t", 0, "q", 0), ("t", 0, "q", 4)), 2: (("t", 0, "q", 8), ("t", 1, "q", 0)),
    3: (("t", 0, "q", 12), ("t", 1, "q", 4)), 4: (("t", 1, "q", 8), ("t", 1, "q", 12)),
    5: (("t", 0, "k", 0), ("t", 0, "k", 4)), 6: (("t", 0, "k", 12), ("t", 0, "k", 8)),
    7: (("t", 1, "k", 0), ("t", 1, "k", 4)), 8: (("t", 1, "k", 8), ("t", 1, "k", 12)), 9: (("s", 0), ("s", 1)),
    10: (("s", 2), ("s", 3), ("s", 4)), 11: (("s", 5), ("s", 6), ("s", 7)), 12: (("s", 8),),
    13: (("s", 9), ("s", 10), ("s", 11)), 14: (("s", 12), ("s", 13)), 15: (("s", 14), ("s", 15)),
}
UNITS = [u for s in sorted(UNITS_AT) for u in UNITS_AT[s]]
MT_STEP = 1
PROJ_AT = {1: ("q", 0), 3: ("q", 1), 5: ("k", 0), 7: ("k", 1)}
ROT_AT = {2: ("q", 0), 4: ("q", 1), 6: ("k", 0), 8: ("k", 1)}
HIGH_AT = {3: ("q", 0), 5: ("q", 1), 6: ("k", 0), 9: ("k", 1)}
XN_STEP, NORM_STEP, XT_STEP, SM_STEP, QK_STEP = 8, 6, 9, 11, 15
BY_DVE = (("t", 0, "q", 0), ("t", 0, "q", 4), ("t", 1, "k", 4), ("t", 1, "q", 4))
INV_STEP = 8
WO_STEP = 9

B_UNITS = len(UNITS) + 1
B_FREES = len(UNITS) // 2
PROJ_UNITS = 4 * NT


def units_until(what):
    return UNITS.index(what) + 1


def by_dve(what):
    return what in BY_DVE


def order_of(side, j):
    return list(PROJ_AT.values()).index((side, j))


def bank_of(what):
    return units_until(what) % 2


def uses_until(what, bank):
    return (units_until(what) + bank) // 2


def at_least(eng, sem, value):
    if isinstance(value, int) and value <= 0:
        return
    eng.wait_ge(sem, value)


def known(b, last=B - 1):
    return not isinstance(b, int) or 0 <= b <= last


class Chain:

    def __init__(self, eng, sem, b, per_batch):
        self.eng, self.sem, self.b, self.per, self.n = eng, sem, b, per_batch, 0

    def add(self, ins):
        self.n += 1
        ins.then_inc(self.sem, 1)
        return self.n

    def need(self, n=None):
        self.eng.wait_ge(self.sem, self.b * self.per + (self.n if n is None else n))


def build(nc, x, W_kv, g_kv, W_kdec, W_vdec, W_q, W_qdec, W_krope, W_qrope, W_o,
          Wg, W1, b1, W2, b2, Ws1, bs1, Ws2, bs2, rope, out):
    x_d = x.rearrange("b (j p) c -> p (b j) c", p=P)
    out_d = out.rearrange("b (j p) c -> p (b j) c", p=P)
    parts_d = nc.dram_tensor("xn_parts", (P, 2, B * T), F32R).ap()

    with ExitStack() as ctx:
        def sb(name, shape, dt):
            return ctx.enter_context(nc.sbuf_tensor(name, shape, dt))

        def sem(name):
            return ctx.enter_context(nc.semaphore(name))

        xres = sb("xres", [P, TILES, C], F32)
        lg = sb("lg", [P, TILES, E], F32)
        with ExitStack() as raw:
            w2 = raw.enter_context(nc.sbuf_tensor("w2", [P, NE, FC, C], F32))
            w1raw = raw.enter_context(nc.sbuf_tensor("w1raw", [P, E, F], F32))
        w2lo = sb("w2lo", [P, NE, FC, C], F32R)
        w2hi = sb("w2hi", [P, E, FC, C], F32R)
        bias1 = sb("bias1", [P, NE * FC], F32)
        b2x = sb("b2x", [2 * NE, C], F32)
        wo = sb("wo", [HD, C], F32)
        wsm = sb("wsm", [P, 2 * P], F32R)
        wkr = sb("wkr", [P, 2, H * DR], F32R)
        wqa = sb("wqa", [2 * RQ, H, D], F32R)
        wqb = sb("wqb", [2 * RQ, H, D], F32R)
        wkv = sb("wkv", [3 * RKV, 2 * HD], F32R)
        ident = sb("ident", [P, P], F32)
        identr = sb("identr", [P, P], F32R)
        identb = sb("identb", [P, P], BF16)
        mask_qk = sb("mask_qk", [P, P], BF16)
        cosx = sb("cosx", [P, NT, D], F32)
        sins = sb("sins", [P, NT, DR], F32)
        QK = sb("QK", [P, 2, 2, H, T], F32R)
        stk = {(s, j): sb(f"stk_{s}{j}", [P, H, KQ if s == "q" else KK], F32R)
               for s in "qk" for j in range(NT)}
        vpad = sb("vpad", [P, NT * H * P + P], F32)
        vraw = sb("vraw", [P, 2, NT, HD], F32)
        prob = sb("prob", [P, 4, 3 * P], F32)
        r = {s: sb(f"rot_{s}", [P, H, D], F32) for s in "qk"}
        t2 = sb("t2", [P, H, DR], F32)
        st6 = sb("st6", [P, NT, 6], F32)
        mv = sb("mv", [P, NT, 2], F32)
        rstd = sb("rstd", [P, NT], F32)
        mhalf = sb("mhalf", [P, NT], F32)
        unit = sb("unit", [P, H], F32)
        pace = sb("pace", [P, 1], F32)
        pace_pool = sb("pace_pool", [P, 1], F32)
        xn = sb("xn", [P, NT, C], F32)
        xhl = sb("xhl", [P, 2, 2, T], F32R)
        smt = sb("smt", [P, NT, SMW], F32)
        sq = sb("sq", [P, NT, RKV], F32)
        ss = sb("ss", [P, NT], F32)
        rs = sb("rs", [P, NT], F32)
        qs = sb("qs", [P, NT, 2, RQ], F32R)
        ks = sb("ks", [P, NT, 3, RKV], F32R)
        qsT = sb("qsT", [2 * RQ, NT, P], F32R)
        ksT = sb("ksT", [3 * RKV, NT, P], F32R)
        mx = sb("mx", [P, 3, H], F32)
        nhl = sb("nhl", [P, NT, 2, H], F32R)
        mT = sb("mT", [2 * H, T], F32R)
        numden = sb("numden", [P, 2, T], F32)
        num, den = numden[:, 0, :], numden[:, 1, :]
        oT = sb("oT", [P, T], F32)
        cw = sb("cw", [P, TILES, NE], F32)
        rsm = sb("rsm", [P, 3, TILES], F32)

        raw_kr = r["q"][:, :, :].rearrange("p h d -> p (h d)")[:, 0:H * DR]
        raw_qr = r["k"][:, :, :].rearrange("p h d -> p (h d)")[:, 0:H * DR]
        raw_sm = t2[:, :, :].rearrange("p h d -> p (h d)")[:, 0:SMW]
        raw_qd = t2[:, :, :].rearrange("p h d -> p (h d)")[:, P:P + HD]
        raw_kv = t2[0:3 * RKV, :, :].rearrange("p h d -> p (h d)")[:, 2 * P:2 * P + 2 * HD]
        g_rep = sq[0:3 * RKV, 0, 0:1]
        kv_hi = qs[0:3 * RKV, :, :, :].rearrange("p j a r -> p (j a r)")
        braw = numden[0:NE * FC, 0, 0:P]

        w1p = QK[:, 0, :, :, :].rearrange("p a h t -> p a (h t)")[:, :, 0:E * F]
        tile512 = lambda n: vpad[:, n * 4 * P:(n + 1) * 4 * P]
        act = [tile512(c) for c in range(FC)]
        w_rep = [tile512(FC + n) for n in range(2)]
        y_w, y_sum = tile512(FC + 2), tile512(FC + 3)
        aparts = QK[:, 1, :, :, :].rearrange("p a h t -> p (a h t)")[:, 0:2 * 2 * FC * 4 * P]\
            .rearrange("p (n a c t) -> p n a c t", n=2, a=2, c=FC)
        xc = [stk["q", n][:, :, :].rearrange("p h k -> p (h k)")[:, 0:2 * 4 * P]
              .rearrange("p (a t) -> p a t", a=2) for n in range(2)]
        ws1 = stk["k", 0][:, :, :].rearrange("p h k -> p (h k)")[:, 0:2 * F].rearrange("p (a f) -> p a f", a=2)
        ws1raw = numden[:, :, :].rearrange("p a t -> p (a t)")
        flat = lambda t: t[:, :, :].rearrange("p h d -> p (h d)")
        w2hi_s = flat(stk["k", 0])[:, 2 * F:3 * F].rearrange("p (c h) -> p c h", c=FC)
        pick = flat(stk["k", 1])[0:2 * NE, 0:NE * P].rearrange("p (e c) -> p e c", e=NE)
        cwT = flat(stk["k", 1])[0:2 * NE, NE * P:NE * P + 4 * P]
        b2p = flat(stk["k", 1])[0:2 * NE, NE * P + 4 * P:NE * P + 6 * P].rearrange("p (a c) -> p a c", a=2)
        cwc = flat(stk["k", 0])[:, 3 * F:3 * F + 2 * 4 * 2 * NE].rearrange("p (n i e) -> p n i e", n=2, i=4)
        cmp_gt = flat(r["q"])[:, 0:8 * E * E].rearrange("p (i a c) -> p i a c", a=E, c=E)
        cmp_eq = flat(r["k"])[:, 0:8 * E * E].rearrange("p (i a c) -> p i a c", a=E, c=E)
        pr = flat(t2)[:, 0:TILES * E].rearrange("p (i e) -> p i e", e=E)
        rank = flat(t2)[:, TILES * E:2 * TILES * E].rearrange("p (i e) -> p i e", e=E)
        tri8 = sb("tri8", [P, E, E], BF16)

        banks = [ctx.enter_context(nc.psum_tensor(f"bank{i}", [P, 512], F32)) for i in range(8)]
        B_PS, ST_PS, PV_PS = banks[2:4], banks[4:6], banks[6:8]


        def diagonal(start):
            return vpad[:, start:start + GH * DIAG].rearrange("p (h c) -> p h c", c=DIAG)[:, :, 0:DC]

        def w1_part(e, part, start, n):
            return w1p[:, part, e * F + start:e * F + start + n] if e < E else ws1[:, part, start:start + n]

        def w2_part(e, part, c):
            if part:
                return w2lo[:, e, c, :]
            return w2hi[:, e, c, :] if e < E else w2hi_s[:, c, :]

        N_X = 4
        XL = TILES // N_X
        s_x = [sem(f"x{n}_loaded") for n in range(N_X)]
        s_wa = sem("attention_weights_loaded")
        s_wr = sem("rope_and_output_weights_loaded")
        s_wb = sem("expert_bias_loaded")
        s_wm = sem("expert_weights_loaded")
        s_const = sem("constants_built")
        s_cast = sem("identities_cast")
        s_init = sem("buffers_preset")
        s_wsplit = sem("attention_weights_split")
        s_biasT = sem("expert_bias_turned")
        s_bias = sem("expert_bias_ready")
        s_xn = sem("xn_ready")
        s_var = sem("variance_ready")
        s_rstd = sem("deviation_inverted")
        s_ms = sem("mean_square_ready")
        s_rs = sem("mean_square_inverted")
        s_xh = sem("xn_high_ready")
        s_xl = sem("xn_low_ready")
        s_xst = [sem(f"xn_parts{i}_stored") for i in range(2)]
        s_smh = sem("small_high_read")
        s_small = sem("small_stacks_ready")
        s_smT = sem("small_stacks_turned")
        s_afill = sem("small_bank_filled")
        s_pfill = sem("projection_bank_filled")
        s_pfree = [sem(f"projection_bank{i}_free") for i in range(2)]
        s_bfill = sem("stack_bank_filled")
        s_bfree = [sem(f"stack_bank{i}_free") for i in range(2)]
        s_rot = {s: sem(f"rotated_{s}") for s in "qk"}
        s_v = sem("values_ready")
        s_hi = {s: sem(f"high_{s}_stacked") for s in "qk"}
        s_dup = {s: sem(f"high_{s}_stacked_again") for s in "qk"}
        s_lo = {s: sem(f"low_{s}_stacked") for s in "qk"}
        s_nm = sem("negative_max_ready")
        s_mT = sem("max_rows_ready")
        s_mrow = sem("max_rows_placed")
        s_st = sem("scores_done")
        s_exp = sem("probs_ready")
        s_masked = sem("probs_masked")
        s_pv = sem("head_values_done")
        s_vp = sem("values_placed")
        s_ev = sem("group_values_read")
        s_oT = sem("attention_normed")
        s_wo = sem("attention_projected")
        s_acc = sem("attention_added")
        c_a = sem("dve_small_steps")
        c_r = sem("dve_rotation_steps")
        c_b = sem("dve_second_tile_maxima")
        c_n = sem("dve_negative_max_high")
        c_c = sem("dve_sum_inverted")
        c_s = sem("dve_setup_steps")
        s_w1h = sem("w1_high_ready")
        s_w1l = sem("w1_low_ready")
        s_ws = sem("shared_weights_loaded")
        c_rt = sem("dve_router_steps")
        s_rt = sem("router_logits_less_max")
        s_exr = sem("router_exp_ready")
        s_cw = sem("chunk_weights_ready")
        s_xc = [sem(f"xn_chunk{i}_loaded") for i in range(2)]
        s_l1 = sem("hidden_done")
        s_act = [sem(f"activation{c}_ready") for c in range(FC)]
        s_ahi = sem("activation_high_ready")
        s_alo = sem("activation_low_ready")
        s_l2 = sem("expert_out_done")
        s_rep = sem("expert_weights_spread")
        s_repc = sem("expert_weights_copied")
        s_yw = sem("expert_out_weighted")
        s_ys = sem("expert_out_added")
        s_cwh = sem("chunk_weights_high_ready")
        s_cwt = sem("chunk_weights_turned")
        s_cwe = sem("chunk_weights_turned_read")
        s_b2 = sem("bias2_done")
        s_b2h = sem("bias2_high_ready")
        s_b2l = sem("bias2_low_ready")
        s_pick = sem("picking_ones_built")
        s_w2h = sem("w2_high_ready")
        s_w2l = sem("w2_low_ready")
        s_tr = sem("chunk_sum_turned")
        s_fin = sem("chunk_sum_added")
        s_out = sem("out_stored")

        block = ctx.enter_context(nc.Block())

        CHUNKS = TILES // 4
        WA_LOADS = 4 + 5
        WM_LOADS = 7

        def run_turns(eng, body):
            for b in (-3, -2, -1, 0, 1):
                body(b, b % 2)
            with eng.Fori(1, 6) as g:
                for par in range(2):
                    body(g * 2 + par, par)
            for b in (12, 13, 14, 15, 16):
                body(b, b % 2)

        def run_chunks(eng, body):
            body(0)
            with eng.Fori(1, CHUNKS // 2) as g:
                body(g)

        def stored_before(b, par):
            return 8 * (b - par)

        def scores_of(b, s):
            return (b, s - SHIFT) if s >= SHIFT else (b - 1, s - SHIFT + H)

        def values_of(b, s):
            return (b, s - SHIFT - PV_LAG) if s >= SHIFT + PV_LAG else (b - 1, s - SHIFT - PV_LAG + H)

        @block.sync
        def _(sp):
            sp.dma_start(xres[:, 0:XL, :], x_d[:, 0:XL, :]).then_inc(s_x[0], 16)
            sp.dma_start(raw_sm[:, 0:RKV], W_kv).then_inc(s_wa, 16)
            sp.dma_start(raw_sm[:, RKV:RKV + RQ], W_q).then_inc(s_wa, 16)
            sp.dma_start(raw_sm[:, RKV + RQ:SMW], Wg).then_inc(s_wa, 16)
            sp.dma_start(raw_kr, W_krope).then_inc(s_wa, 16)
            for dst, src, n in ((raw_qr, W_qrope, 2), (raw_qd, W_qdec, 2), (raw_kv[:, 0:HD], W_kdec, 3),
                                (raw_kv[:, HD:2 * HD], W_vdec, 3), (g_rep, g_kv.rearrange("(r a) -> r a", a=1), 3)):
                rows, cols = src.shape
                sp.dma_start(dst[0:n * rows, :], src.unsqueeze(0).to_broadcast([n, rows, cols])).then_inc(s_wa, 16)
            rope_v = rope.rearrange("(j p) c -> p j c", p=P)
            sp.dma_start(cosx[:, :, :], rope_v[:, :, 0:D]).then_inc(s_wr, 16)
            sp.dma_start(sins[:, :, :], rope_v[:, :, D:D + DR]).then_inc(s_wr, 16)
            sp.dma_start(wo[:, :], W_o).then_inc(s_wr, 16)
            for n in range(1, N_X):
                sp.dma_start(xres[:, n * XL:(n + 1) * XL, :], x_d[:, n * XL:(n + 1) * XL, :]).then_inc(s_x[n], 16)
            sp.dma_start(braw[0:E * FC, :], b1.rearrange("e (c p) -> (e c) p", p=P)).then_inc(s_wb, 16)
            sp.dma_start(braw[E * FC:NE * FC, :], bs1.rearrange("(c p) -> c p", p=P)).then_inc(s_wb, 16)
            sp.dma_start(w1raw[:, 0:E, :], W1.rearrange("e h f -> h e f")).then_inc(s_wm, 16)
            sp.dma_start(w2[:, 0:E, :, :], W2.rearrange("e (c p) h -> p e c h", p=P)).then_inc(s_wm, 16)
            sp.dma_start(w2[:, E, :, :], Ws2.rearrange("(c p) h -> p c h", p=P)).then_inc(s_wm, 16)
            for n in range(0, 2 * NE, NE):
                sp.dma_start(b2x[n:n + E, :], b2).then_inc(s_wm, 16)
                sp.dma_start(b2x[n + E:n + NE, :], bs2.rearrange("(a h) -> a h", a=1)).then_inc(s_wm, 16)

            def turn(b, par):
                if known(b):
                    sp.wait_ge(s_mT, b + 1)
                    sp.dma_start(QK[KQ:KK, par, 0, :, :].bitcast(F32), mT[:, :].bitcast(F32)).then_inc(s_mrow, 16)
                if known(b + 3):
                    at = slice((b + 3) * T, (b + 4) * T) if isinstance(b, int) else bass.ds(sp.snap((b + 3) * T), T)
                    sp.wait_ge(s_xh, b + 4)
                    sp.wait_ge(s_xl, b + 4)
                    sp.wait_ge(s_x[0], 16)
                    sp.dma_start(parts_d[:, :, at].bitcast(F32), xhl[:, (par + 1) % 2, :, :].bitcast(F32)).then_inc(s_xst[(par + 1) % 2], 16)

            run_turns(sp, turn)

            for i in range(2):
                sp.wait_ge(s_xst[i], 8 * B)
            sp.wait_ge(s_bfill, B * B_UNITS)

            def load_chunk(n, at):
                sp.dma_start(xc[n].bitcast(F32), parts_d[:, :, at].bitcast(F32)).then_inc(s_xc[n], 16)

            def store_chunk(g, n):
                at = slice((2 * g + n) * 4, (2 * g + n + 1) * 4) if isinstance(g, int) else \
                    bass.ds(sp.snap(g * 8 + 4 * n), 4)
                sp.wait_ge(s_fin, g * 2 + n + 1)
                sp.wait_ge(s_x[0], 16)
                sp.dma_start(out_d[:, at, :], xres[:, at, :]).then_inc(s_out, 16)

            for n in range(2):
                load_chunk(n, slice(n * 4 * P, (n + 1) * 4 * P))
            sp.wait_ge(s_oT, B)
            sp.dma_start(ws1raw, Ws1).then_inc(s_ws, 16)
            with sp.Fori(0, CHUNKS // 2 - 1) as g:
                for n in range(2):
                    store_chunk(g, n)
                    at = bass.ds(sp.snap((g * 2 + n + 2) * (4 * P)), 4 * P)
                    sp.wait_ge(s_l1, (g * 2 + n + 1) * (NE * FC))
                    sp.wait_ge(s_x[0], 16)
                    load_chunk(n, at)
            for n in range(2):
                store_chunk(CHUNKS // 2 - 1, n)
            sp.wait_ge(s_out, 16 * CHUNKS)

        @block.gpsimd
        def _(pool):
            nc.gpsimd.memset(ident[:, :], 0.0).then_inc(s_const, 1)
            nc.gpsimd.memset(mask_qk[:, :], 0.0).then_inc(s_const, 1)
            nc.gpsimd.memset(tri8[:, :, :], 1.0).then_inc(s_const, 1)
            pool.wait_ge(s_const, 3)
            nc.gpsimd.affine_select(out=ident[:, :], in_=ident[:, :], compare_op=ALU.not_equal, fill=1.0,
                                    base=0, pattern=[[-1, P]], channel_multiplier=1).then_inc(s_const, 1)
            nc.gpsimd.affine_select(out=mask_qk[:, :], in_=mask_qk[:, :], compare_op=ALU.is_ge, fill=NEG,
                                    base=0, pattern=[[-1, P]], channel_multiplier=1).then_inc(s_const, 1)
            nc.gpsimd.affine_select(out=tri8[:, :, :], in_=tri8[:, :, :], compare_op=ALU.is_gt, fill=0.0,
                                    base=0, pattern=[[1, E], [-1, E]], channel_multiplier=0).then_inc(s_const, 1)
            nc.gpsimd.memset(vpad[:, :], 0.0).then_inc(s_init, 1)
            pool.wait_ge(s_init, 1)
            for n in range(NT * 2):
                ones = diagonal(n * GH * P + GW)
                nc.gpsimd.memset(ones, 1.0).then_inc(s_init, 1)
            for j in range(NT):
                nc.gpsimd.memset(stk["k", j][:, :, KQ:KK].bitcast(F32), 1.0).then_inc(s_init, 1)
            nc.gpsimd.memset(wsm[:, :].bitcast(F32), 0.0).then_inc(s_init, 1)
            nc.gpsimd.memset(wqb[:, :, :].bitcast(F32), 0.0).then_inc(s_init, 1)
            nc.gpsimd.memset(cw[:, :, E:NE], 0.1).then_inc(s_init, 1)
            nc.gpsimd.memset(mhalf[:, :], -0.5).then_inc(s_init, 1)
            nc.gpsimd.memset(unit[:, :], 1.0).then_inc(s_init, 1)
            pool.wait_ge(s_init, INIT)

            def place(b, g, par):
                if g == 0:
                    pool.wait_ge(s_v, NT * (b + 1))
                at_least(pool, s_pv, (b - 1) * H + (g + 1) * GH)
                for j in range(NT):
                    nc.gpsimd.tensor_tensor(
                        diagonal((j * H + g * GH) * P),
                        vraw[:, par, j, g * GW:(g + 1) * GW].rearrange("p (h d) -> p h d", d=DC),
                        unit[:, 0:GH].unsqueeze(2).to_broadcast([P, GH, DC]), ALU.mult).then_inc(s_vp, 1)

            def stack_low(b, side, j):
                low = 2 if side == "q" else 1
                pool.wait_ge(s_hi[side], b * NT + j + 1)
                nc.gpsimd.tensor_tensor(stk[side, j][:, :, low * D:(low + 1) * D], r[side][:, :, :],
                                        stk[side, j][:, :, 0:D], ALU.subtract).then_inc(s_lo[side], 1)

            def stack_again(b, side, j):
                again = 1 if side == "q" else 2
                pool.wait_ge(s_hi[side], b * NT + j + 1)
                nc.gpsimd.tensor_tensor(stk[side, j][:, :, again * D:(again + 1) * D], stk[side, j][:, :, 0:D],
                                        unit[:, :].unsqueeze(2).to_broadcast([P, H, D]), ALU.mult).then_inc(s_dup[side], 1)

            def turn(b, par):
                for s in range(STEPS):
                    bb, h = scores_of(b, s)
                    if known(bb):
                        at_least(pool, s_masked, bb * H + h)
                        pool.wait_ge(s_exp, bb * H + h + 1)
                        nc.gpsimd.tensor_tensor(pace_pool[:, :], unit[:, 0:1], unit[:, 0:1], ALU.mult)
                        blocks = prob[:, h % 4, :].rearrange("p (a q) -> p a q", a=3)[:, 0:3:2, :]
                        nc.gpsimd.affine_select(out=blocks, in_=blocks, compare_op=ALU.is_ge, fill=0.0, base=0,
                                                pattern=[[0, 2], [1, P]], channel_multiplier=-1).then_inc(s_masked, 1)
                    if known(b) and s == 0:
                        place(b, 0, par)
                    if known(b) and s == SHIFT + PV_LAG - 1:
                        place(b, 1, par)
                    if known(b + 2) and s in HIGH_AT:
                        stack_low(b + 2, *HIGH_AT[s])
                    if known(b + 2) and s - 1 in HIGH_AT:
                        stack_again(b + 2, *HIGH_AT[s - 1])
                    if known(b + 3) and s == NORM_STEP:
                        pool.wait_ge(s_var, b + 4)
                        nc.gpsimd.tensor_tensor(rstd[:, :], rstd[:, :], mhalf[:, :], ALU.pow).then_inc(s_rstd, 1)
                    if known(b + 3) and s == SM_STEP + 1:
                        pool.wait_ge(s_ms, b + 4)
                        nc.gpsimd.tensor_tensor(rs[:, :], rs[:, :], mhalf[:, :], ALU.pow).then_inc(s_rs, 1)

            run_turns(pool, turn)

            pool.wait_ge(s_bfill, B * B_UNITS)
            nc.gpsimd.memset(pick.bitcast(F32), 0.0).then_inc(s_pick, 1)
            for n in range(2):
                pool.wait_ge(s_pick, n + 1)
                nc.gpsimd.affine_select(out=pick, in_=pick.bitcast(F32), compare_op=ALU.not_equal, fill=1.0,
                                        base=-n * NE, pattern=[[-1, NE], [0, P]], channel_multiplier=1).then_inc(s_pick, 1)

        @block.scalar
        def _(sc):
            act_f = nc.scalar.activation
            sc.wait_ge(s_const, 6)
            act_f(identr[:, :], ident[:, :], ACT.Copy).then_inc(s_cast, 1)
            act_f(identb[:, :], ident[:, :], ACT.Copy).then_inc(s_cast, 1)

            def turn(b, par):
                for s in range(STEPS):
                    bb, h = scores_of(b, s)
                    if known(bb):
                        n = bb * H + h
                        sc.wait_ge(s_st, n + 1)
                        at_least(sc, s_pv, n - 3)
                        act_f(prob[:, h % 4, :], ST_PS[h % 2][:, 0:3 * P], ACT.Exp, scale=SCALE).then_inc(s_exp, 1)
                    bb, h = values_of(b, s)
                    if known(bb) and h % GH == GH - 1:
                        g = h // GH
                        rows = slice(g * GW, (g + 1) * GW)
                        sc.wait_ge(s_pv, bb * H + h + 1)
                        at_least(sc, s_oT, bb)
                        act_f(num[rows], PV_PS[g][0:GW, 0:T], ACT.Copy).then_inc(s_ev, 1)
                        act_f(den[rows], PV_PS[g][GW:2 * GW, 0:T], ACT.Copy).then_inc(s_ev, 1)
                    if isinstance(b, int) and b == -1 and s == 0:
                        sc.wait_ge(s_biasT, 1)
                        act_f(bias1[:, :], banks[1][:, 0:NE * FC], ACT.Copy).then_inc(s_bias, 1)
                    if s == MT_STEP and known(b):
                        sc.wait_ge(s_bfill, (b + 1) * B_UNITS)
                        at_least(sc, s_mrow, 16 * b)
                        act_f(mT[:, :], B_PS[0][0:2 * H, 0:T], ACT.Copy).then_inc(s_mT, 1)
                    if known(b + 1):
                        for what in UNITS_AT.get(s, ()):
                            if what[0] == "s" or by_dve(what):
                                continue
                            _, j, side, h0 = what
                            rows = KK if side == "k" else KQ
                            bank = bank_of(what)
                            sc.wait_ge(s_bfill, (b + 1) * B_UNITS + units_until(what))
                            at_least(sc, s_st, (b - 1) * H + h0 + 4)
                            act_f(QK[0:rows, (par + 1) % 2, "qk".index(side), h0:h0 + 4, j * P:(j + 1) * P],
                                  B_PS[bank][0:rows, :].rearrange("p (h t) -> p h t", h=4),
                                  ACT.Copy).then_inc(s_bfree[bank], 1)
                    if known(b + 2) and s in ROT_AT:
                        side, j = ROT_AT[s]
                        n = (b + 2) * NT + j
                        if side == "k":
                            sc.wait_ge(s_pfill, (b + 2) * PROJ_UNITS + 2 * order_of(side, j) + 1)
                            at_least(sc, s_vp, 2 * NT * (b + 1))
                            act_f(vraw[:, par, j, :], banks[0][:, HD:2 * HD], ACT.Copy).then_inc(s_v, 1)
                            at_least(sc, s_lo["k"], n)
                            act_f(r["k"][:, :, 0:DC], banks[0][:, 0:HD].rearrange("p (h d) -> p h d", h=H),
                                  ACT.Copy).then_inc(s_pfree[0], 1)
                    if known(b + 2) and s in HIGH_AT:
                        side, j = HIGH_AT[s]
                        n = (b + 2) * NT + j
                        if side == "k":
                            sc.wait_ge(s_pfree[0], (b + 2) * 4 + order_of(side, j) + 1)
                        sc.wait_ge(s_rot[side], n + 1)
                        at_least(sc, s_bfill, (b + 1) * B_UNITS + units_until(("t", j, side, H - 4)) if known(b + 1) else 0)
                        act_f(stk[side, j][:, :, 0:D], r[side][:, :, :], ACT.Copy).then_inc(s_hi[side], 1)
                    if known(b + 3) and s == XT_STEP:
                        sc.wait_ge(s_afill, (b + 3) * 3 + 1)
                        at_least(sc, s_xst[(par + 1) % 2], stored_before(b + 3, (par + 1) % 2))
                        at_least(sc, s_pfill, (b + 2) * PROJ_UNITS)
                        act_f(xhl[:, (par + 1) % 2, 0, :], banks[0][:, 0:T], ACT.Copy).then_inc(s_xh, 1)
                    if known(b + 3) and s == SM_STEP:
                        sc.wait_ge(s_afill, (b + 3) * 3 + 2)
                        at_least(sc, s_small, b + 3)
                        act_f(smt[:, :, :], banks[1][:, :].rearrange("p (j c) -> p j c", j=NT)[:, :, 0:SMW],
                              ACT.Copy).then_inc(s_smh, 1)
                    if known(b + 3) and s == QK_STEP:
                        sc.wait_ge(s_afill, (b + 3) * 3 + 3)
                        at_least(sc, s_pfill, (b + 3) * PROJ_UNITS)
                        act_f(qsT[:, :, :], banks[0][:, 0:T].rearrange("p (j t) -> p j t", j=NT),
                              ACT.Copy).then_inc(s_smT, 1)
                        act_f(ksT[:, :, :], banks[0][0:3 * RKV, T:2 * T].rearrange("p (j t) -> p j t", j=NT),
                              ACT.Copy).then_inc(s_smT, 1)
                    if isinstance(b, int) and b == B - 2 and s == 1:
                        sc.wait_ge(s_rt, 1)
                        act_f(pr, pr, ACT.Exp).then_inc(s_exr, 1)
                    if isinstance(b, int) and b == B - 1:
                        if 5 <= s < 5 + E:
                            e = s - 5
                            if e == 0:
                                sc.wait_ge(s_wm, 16 * WM_LOADS)
                                sc.wait_ge(s_st, (B - 1) * H)
                            act_f(w1_part(e, 0, 0, F), w1raw[:, e, :], ACT.Copy).then_inc(s_w1h, 1)
                        if 7 <= s:
                            for e in ((s - 7,) if s < STEPS - 1 else (E, )):
                                dst = w2hi[:, e, :, :] if e < E else w2hi_s
                                if e < E:
                                    sc.wait_ge(s_w1l, e + 1)
                                else:
                                    sc.wait_ge(s_bfill, B * B_UNITS)
                                act_f(dst, w2[:, e, :, :], ACT.Copy).then_inc(s_w2h, 1)

            run_turns(sc, turn)


            def copy_spread(M, slot):
                sc.wait_ge(s_rep, M + 1)
                at_least(sc, s_yw, M - 1)
                act_f(w_rep[slot], banks[6][:, :], ACT.Copy).then_inc(s_repc, 1)

            def chunks(g):
                for n in range(2):
                    for e in range(NE):
                        m = n * NE + e
                        M = g * (2 * NE) + m
                        for c in range(FC):
                            k = e * FC + c
                            sc.wait_ge(s_l1, M * FC + c + 1)
                            at_least(sc, s_alo, (M - 1) * FC + c + 1)
                            act_f(act[c], banks[c][:, :], ACT.Silu, bias=bias1[:, k:k + 1]).then_inc(s_act[c], 1)
                            for d in ((), (0,), (1,), (2, 3))[c]:
                                if d == 0:
                                    at_least(sc, s_l2, M - 1)
                                sc.wait_ge(s_act[d], M + 1)
                                act_f(aparts[:, m % 2, 0, d, :], act[d], ACT.Copy).then_inc(s_ahi, 1)
                        if e == 0:
                            sc.wait_ge(s_cwt, g * 2 + n + 1)
                            act_f(cwT, banks[7][0:2 * NE, :], ACT.Copy).then_inc(s_cwe, 1)
                        if e > 0:
                            copy_spread(M - 1, (m - 1) % 2)
                        if isinstance(g, int) and m == 1:
                            sc.wait_ge(s_ws, 16)
                            act_f(w1_part(E, 0, 0, F), ws1raw, ACT.Copy).then_inc(s_w1h, 1)
                    copy_spread(g * (2 * NE) + (n + 1) * NE - 1, ((n + 1) * NE - 1) % 2)

            run_chunks(sc, chunks)

        @block.vector
        def _(dve):
            V = nc.vector

            steps = Chain(dve, c_s, 0, 0)
            dve.wait_ge(s_wa, 16 * WA_LOADS)
            dve.wait_ge(s_init, INIT)
            steps.add(V.tensor_scalar(raw_kv, raw_kv, g_rep, None, ALU.mult))
            steps.add(V.tensor_copy(wsm[:, 0:SMW], raw_sm))
            steps.add(V.tensor_copy(wkr[:, 0, :], raw_kr))
            steps.add(V.tensor_copy(wqa[:, :, 0:DC], raw_qd.rearrange("p (h d) -> p h d", h=H)))
            steps.add(V.tensor_copy(wqa[:, :, DC:D], raw_qr.rearrange("p (h d) -> p h d", h=H)))
            steps.need()
            steps.add(V.tensor_copy(kv_hi, raw_kv))
            steps.add(V.tensor_tensor(wsm[:, P:P + SMW], raw_sm, wsm[:, 0:SMW], ALU.subtract))
            steps.add(V.tensor_tensor(wkr[:, 1, :], raw_kr, wkr[:, 0, :], ALU.subtract))
            steps.add(V.tensor_tensor(wqb[0:RQ, :, 0:DC], raw_qd[0:RQ, :].rearrange("p (h d) -> p h d", h=H),
                                      wqa[0:RQ, :, 0:DC], ALU.subtract))
            steps.add(V.tensor_tensor(wqb[0:RQ, :, DC:D], raw_qr[0:RQ, :].rearrange("p (h d) -> p h d", h=H),
                                      wqa[0:RQ, :, DC:D], ALU.subtract))
            steps.need()
            steps.add(V.tensor_copy(wkv[0:2 * RKV, :], raw_kv[0:2 * RKV, :]))
            steps.need()
            V.tensor_tensor(wkv[2 * RKV:3 * RKV, :], raw_kv[2 * RKV:3 * RKV, :], kv_hi[2 * RKV:3 * RKV, :],
                            ALU.subtract).then_inc(s_wsplit, 1)
            dve.wait_ge(s_wsplit, 1)

            dve.wait_ge(s_wr, 16 * 3)

            def normalise(b, steps):
                i = b * NT
                at_least(dve, c_a, b * SMALL_STEPS)
                at_least(dve, s_xn, b * NT)
                for n in range(N_X):
                    if not isinstance(b, int) or n == i // XL:
                        dve.wait_ge(s_x[n], 16)
                for j in range(NT):
                    at = slice(i + j, i + j + 1) if isinstance(b, int) else bass.ds(i + j, 1)
                    steps.add(V.bn_stats(st6[:, j, :], xres[:, at, :]))
                steps.need()
                steps.add(V.memset(pace[:, :], 0.0))
                for j in range(NT):
                    steps.add(V.bn_aggr(mv[:, j, :], st6[:, j, :]))
                steps.need()
                V.tensor_scalar(rstd[:, :], mv[:, :, 1], LN_EPS, None, ALU.add).then_inc(s_var, 1)

            def normalised(b):
                i = b * NT
                dve.wait_ge(s_rstd, b + 1)
                at_least(dve, s_afill, 3 * b - 2)
                for j in range(NT):
                    at = slice(i + j, i + j + 1) if isinstance(b, int) else bass.ds(i + j, 1)
                    V.tensor_scalar(xn[:, j:j + 1, :], xres[:, at, :], mv[:, j, 0:1], rstd[:, j:j + 1],
                                    ALU.subtract, ALU.mult).then_inc(s_xn, 1)

            def small_products(b, steps):
                low = banks[1][:, :].rearrange("p (j c) -> p j c", j=NT)
                dve.wait_ge(s_smh, b + 1)
                at = slice(b * NT, (b + 1) * NT) if isinstance(b, int) else bass.ds(b * NT, NT)
                steps.add(V.tensor_tensor(lg[:, at, :], low[:, :, P + RKV + RQ:P + SMW], smt[:, :, RKV + RQ:SMW], ALU.add))
                steps.add(V.tensor_tensor(smt[:, :, 0:RKV + RQ], low[:, :, P:P + RKV + RQ],
                                          smt[:, :, 0:RKV + RQ], ALU.add))
                steps.need()
                kv, qc = smt[:, :, 0:RKV], smt[:, :, RKV:RKV + RQ]
                steps.add(V.tensor_tensor(sq[:, :, :], kv, kv, ALU.mult))
                at_least(dve, s_afill, 3 * b)
                steps.add(V.tensor_copy(qs[:, :, 0, :], qc))
                steps.need()
                steps.add(V.tensor_reduce(ss[:, :], sq[:, :, :], AX.X, ALU.add))
                steps.need()
                V.tensor_scalar(rs[:, :], ss[:, :], 1.0 / RKV, RMS_EPS, ALU.mult, ALU.add).then_inc(s_ms, 1)

            def small_stacks(b, steps):
                kv, qc = smt[:, :, 0:RKV], smt[:, :, RKV:RKV + RQ]
                dve.wait_ge(s_rs, b + 1)
                steps.add(V.tensor_tensor(kv, kv, rs[:, :].unsqueeze(2).to_broadcast([P, NT, RKV]), ALU.mult))
                steps.need()
                steps.add(V.tensor_copy(ks[:, :, 0:3:2, :], kv.unsqueeze(2).to_broadcast([P, NT, 2, RKV])))
                steps.need()
                steps.add(V.tensor_tensor(ks[:, :, 1, :], kv, ks[:, :, 0, :], ALU.subtract))
                V.tensor_tensor(qs[:, :, 1, :], qc, qs[:, :, 0, :], ALU.subtract).then_inc(s_small, 1)

            def rotate(b, side, j, steps):
                n = b * NT + j
                out = r[side]
                at_least(dve, s_hi[side], n)
                at_least(dve, s_lo[side], n)
                order = order_of(side, j)
                for other in "qk":
                    at_least(dve, s_rot[other], b * NT + sum(order_of(other, i) < order for i in range(NT)))
                if side == "q":
                    for half in range(2):
                        hs = slice(half * GH, (half + 1) * GH)
                        bank = 1 - half
                        dve.wait_ge(s_pfill, b * PROJ_UNITS + 2 * order + half + 1)
                        ps = banks[bank][:, 0:GH * D].rearrange("p (h d) -> p h d", h=GH)
                        steps.add(V.tensor_tensor(out[:, hs, :], ps,
                                                  cosx[:, j, :].unsqueeze(1).to_broadcast([P, GH, D]), ALU.mult))
                        turned(ps[:, :, DC:D], hs, j, steps, bank)
                else:
                    dve.wait_ge(s_pfill, b * PROJ_UNITS + 2 * order + 2)
                    ps = banks[1][:, :].rearrange("p (h d) -> p h d", h=H)
                    steps.add(V.tensor_tensor(out[:, :, DC:D], ps,
                                              cosx[:, j, DC:D].unsqueeze(1).to_broadcast([P, H, DR]), ALU.mult))
                    turned(ps, slice(0, H), j, steps, 1)
                steps.need()
                dve.wait_ge(s_pfree[1], b * 4 + order + 1)
                if side == "q":
                    dve.wait_ge(s_pfree[0], b * 4 + order + 1)
                V.tensor_tensor(out[:, :, DC:D], out[:, :, DC:D], t2[:, :, :], ALU.add).then_inc(s_rot[side], 1)

            def turned(ps, hs, j, steps, bank):
                hh, n = DR // 2, hs.stop - hs.start
                steps.add(V.tensor_tensor(t2[:, hs, 0:hh], ps[:, :, hh:DR],
                                          sins[:, j, 0:hh].unsqueeze(1).to_broadcast([P, n, hh]), ALU.mult))
                V.tensor_tensor(t2[:, hs, hh:DR], ps[:, :, 0:hh],
                                sins[:, j, hh:DR].unsqueeze(1).to_broadcast([P, n, hh]), ALU.mult)\
                    .then_inc(s_pfree[bank], 1)

            def place_stack(b, what, par):
                _, j, side, h0 = what
                rows = KK if side == "k" else KQ
                bank = bank_of(what)
                dve.wait_ge(s_bfill, b * B_UNITS + units_until(what))
                at_least(dve, s_st, (b - 2) * H + h0 + 4)
                V.tensor_copy(QK[0:rows, par, "qk".index(side), h0:h0 + 4, j * P:(j + 1) * P],
                              B_PS[bank][0:rows, :].rearrange("p (h t) -> p h t", h=4)).then_inc(s_bfree[bank], 1)

            router_steps = Chain(dve, c_rt, 0, 0)

            def router(part):
                steps = router_steps
                bc = lambda t: t.unsqueeze(2).to_broadcast([P, TILES, E])
                top, tot, inv = rsm[:, 0, :], rsm[:, 1, :], rsm[:, 2, :]
                if part == 0:
                    dve.wait_ge(c_a, B * SMALL_STEPS)
                    for side in "qk":
                        dve.wait_ge(s_rot[side], TILES)
                        dve.wait_ge(s_hi[side], TILES)
                        dve.wait_ge(s_lo[side], TILES)
                    steps.add(V.tensor_reduce(top, lg[:, :, :], AX.X, ALU.max))
                    steps.need()
                    V.tensor_tensor(pr, lg[:, :, :], bc(top), ALU.subtract).then_inc(s_rt, 1)
                elif part == 1:
                    dve.wait_ge(s_exr, 1)
                    steps.add(V.tensor_reduce(tot, pr, AX.X, ALU.add))
                    steps.need()
                    steps.add(V.reciprocal(inv, tot))
                    steps.need()
                    steps.add(V.tensor_tensor(pr, pr, bc(inv), ALU.mult))
                    steps.need()
                elif part < 2 + TILES // 8:
                    q = part - 2
                    ts = slice(8 * q, 8 * q + 8)
                    mine = pr[:, ts, :].unsqueeze(3).to_broadcast([P, 8, E, E])
                    other = pr[:, ts, :].unsqueeze(2).to_broadcast([P, 8, E, E])
                    steps.add(V.tensor_tensor(cmp_gt, other, mine, ALU.is_gt))
                    steps.add(V.tensor_tensor(cmp_eq, other, mine, ALU.is_equal))
                    steps.need()
                    steps.add(V.tensor_tensor(cmp_eq, cmp_eq, tri8[:, :, :].unsqueeze(1).to_broadcast([P, 8, E, E]), ALU.mult))
                    steps.need()
                    steps.add(V.tensor_tensor(cmp_gt, cmp_gt, cmp_eq, ALU.add))
                    steps.need()
                    steps.add(V.tensor_reduce(rank[:, ts, :], cmp_gt, AX.X, ALU.add))
                    steps.need()
                else:
                    steps.add(V.tensor_scalar(rank, rank, 2.0, None, ALU.is_lt))
                    steps.need()
                    steps.add(V.tensor_tensor(pr, pr, rank, ALU.mult))
                    steps.need()
                    steps.add(V.tensor_reduce(tot, pr, AX.X, ALU.add))
                    steps.need()
                    steps.add(V.tensor_scalar(tot, tot, TOP_EPS, None, ALU.add))
                    steps.need()
                    steps.add(V.reciprocal(inv, tot))
                    steps.need()
                    steps.add(V.tensor_tensor(cw[:, :, 0:E], pr, bc(inv), ALU.mult))
                    steps.need()

            def turn(b, par):
                small = Chain(dve, c_a, b + 3, SMALL_STEPS)
                rot = Chain(dve, c_r, b + 2, ROT_STEPS)
                for s in range(STEPS):
                    if known(b - 1) and s == INV_STEP:
                        dve.wait_ge(s_ev, 4 * b)
                        V.reciprocal(den, den).then_inc(c_c, 1)
                        dve.wait_ge(c_c, b)
                        at_least(dve, s_wo, b - 1)
                        V.tensor_tensor(oT[:, :], num, den, ALU.mult).then_inc(s_oT, 1)
                    if known(b - 1) and s == WO_STEP + 1:
                        dve.wait_ge(s_wo, b)
                        at = slice((b - 1) * NT, b * NT) if isinstance(b, int) else bass.ds((b - 1) * NT, NT)
                        V.tensor_tensor(xres[:, at, :], PV_PS[1][:, 0:T].rearrange("p (j c) -> p j c", j=NT),
                                        xres[:, at, :], ALU.add).then_inc(s_acc, 1)
                    if known(b + 2) and s in ROT_AT:
                        rotate(b + 2, *ROT_AT[s], rot)
                    if known(b + 1):
                        for what in UNITS_AT.get(s, ()):
                            if by_dve(what):
                                place_stack(b + 1, what, (par + 1) % 2)
                        for what in UNITS_AT.get(s, ()):
                            if what[0] == "t":
                                continue
                            h, bank = what[1], bank_of(what)
                            dve.wait_ge(s_bfill, (b + 1) * B_UNITS + units_until(what))
                            ps = B_PS[bank]
                            V.tensor_reduce(mx[:, :, h], ps[:, 0:3 * P].rearrange("p (a c) -> p a c", a=3),
                                            AX.X, ALU.max).then_inc(s_bfree[bank], 1)
                        if s == max(UNITS_AT):
                            for i in range(2):
                                dve.wait_ge(s_bfree[i], (b + 2) * B_FREES)
                            V.tensor_tensor(mx[:, 1, :], mx[:, 1, :], mx[:, 2, :], ALU.max).then_inc(c_b, 1)
                            dve.wait_ge(c_b, b + 2)
                            at_least(dve, s_bfill, (b + 1) * B_UNITS)
                            V.tensor_scalar(nhl[:, :, 0, :], mx[:, 0:NT, :], -1.0, None, ALU.mult).then_inc(c_n, 1)
                            dve.wait_ge(c_n, b + 2)
                            V.scalar_tensor_tensor(out=nhl[:, :, 1, :], in0=mx[:, 0:NT, :], scalar=-1.0,
                                                   in1=nhl[:, :, 0, :], op0=ALU.mult, op1=ALU.subtract).then_inc(s_nm, 1)
                    if known(b + 3):
                        if s == NORM_STEP:
                            normalise(b + 3, small)
                        if s == XN_STEP:
                            normalised(b + 3)
                        if s == XT_STEP + 1:
                            dve.wait_ge(s_xh, b + 4)
                            V.tensor_tensor(xhl[:, (par + 1) % 2, 1, :], banks[0][:, 0:T], xhl[:, (par + 1) % 2, 0, :],
                                            ALU.subtract).then_inc(s_xl, 1)
                        if s == SM_STEP:
                            small_products(b + 3, small)
                        if s == SM_STEP + 2:
                            small_stacks(b + 3, small)
                    if isinstance(b, int) and b == B - 2 and s % 2 == 0 and s // 2 < 3 + TILES // 8:
                        router(s // 2)
                    if isinstance(b, int) and b == B - 1:
                        if 5 <= s < 5 + E:
                            e = s - 5
                            dve.wait_ge(s_w1h, e + 1)
                            V.tensor_tensor(w1_part(e, 1, 0, F), w1raw[:, e, :], w1_part(e, 0, 0, F),
                                            ALU.subtract).then_inc(s_w1l, 1)
                        if s >= 8:
                            w2_low(s - 8)
                assert not known(b + 3) or small.n == SMALL_STEPS, small.n
                assert not known(b + 2) or rot.n == ROT_STEPS, rot.n

            def w2_low(e):
                dve.wait_ge(s_w2h, e + 1)
                high = w2hi[:, e, :, :] if e < E else w2hi_s
                V.tensor_tensor(w2lo[:, e, :, :], w2[:, e, :, :], high, ALU.subtract).then_inc(s_w2l, 1)

            run_turns(dve, turn)
            w2_low(E)

            dve.wait_ge(s_acc, B)
            dve.wait_ge(s_wm, 16 * WM_LOADS)
            dve.wait_ge(s_bfill, B * B_UNITS)
            V.tensor_copy(b2p[:, 0, :], b2x[:, :]).then_inc(s_b2h, 1)
            dve.wait_ge(s_b2h, 1)
            V.tensor_tensor(b2p[:, 1, :], b2x[:, :], b2p[:, 0, :], ALU.subtract).then_inc(s_b2l, 1)

            def add_expert(g, n, e):
                m = n * NE + e
                M = g * (2 * NE) + m
                dve.wait_ge(s_l2, M + 1)
                dve.wait_ge(s_repc, M + 1)
                at_least(dve, s_ys, M)
                V.tensor_tensor(y_w, banks[4 + m % 2][:, :], w_rep[m % 2], ALU.mult).then_inc(s_yw, 1)
                dve.wait_ge(s_yw, M + 1)
                if e == 0:
                    dve.wait_ge(s_b2, g * 2 + n + 1)
                    at_least(dve, s_tr, g * 2 + n)
                V.tensor_tensor(y_sum, y_w, banks[7][:, :] if e == 0 else y_sum, ALU.add).then_inc(s_ys, 1)

            def finish(g, n):
                chunk = slice(g * 8 + 4 * n, g * 8 + 4 * n + 4) if isinstance(g, int) else bass.ds(g * 8 + 4 * n, 4)
                dve.wait_ge(s_tr, g * 2 + n + 1)
                V.tensor_tensor(xres[:, chunk, :], banks[7][:, :].rearrange("p (i c) -> p i c", i=4),
                                xres[:, chunk, :], ALU.add).then_inc(s_fin, 1)

            def chunks(g):
                for n in range(2):
                    chunk = slice(g * 8 + 4 * n, g * 8 + 4 * n + 4) if isinstance(g, int) else bass.ds(g * 8 + 4 * n, 4)
                    at_least(dve, s_cwt, g * 2 + n - 1)
                    V.tensor_copy(cwc[:, n, :, 0:NE], cw[:, chunk, :]).then_inc(s_cwh, 1)
                    dve.wait_ge(s_cwh, g * 2 + n + 1)
                    V.tensor_tensor(cwc[:, n, :, NE:2 * NE], cw[:, chunk, :], cwc[:, n, :, 0:NE],
                                    ALU.subtract).then_inc(s_cw, 1)
                    for e in range(NE):
                        m = n * NE + e
                        M = g * (2 * NE) + m
                        for c in range(FC):
                            dve.wait_ge(s_ahi, M * FC + c + 1)
                            V.tensor_tensor(aparts[:, m % 2, 1, c, :], act[c], aparts[:, m % 2, 0, c, :],
                                            ALU.subtract).then_inc(s_alo, 1)
                        if e == 0 and n == 1:
                            finish(g, 0)
                        if e == 0 and n == 0 and not isinstance(g, int):
                            finish(g - 1, 1)
                        if e > 0:
                            add_expert(g, n, e - 1)
                        if isinstance(g, int) and m == 1:
                            dve.wait_ge(s_w1h, NE)
                            V.tensor_tensor(w1_part(E, 1, 0, F), ws1raw, w1_part(E, 0, 0, F),
                                            ALU.subtract).then_inc(s_w1l, 1)
                    add_expert(g, n, NE - 1)

            run_chunks(dve, chunks)
            finish(CHUNKS // 2 - 1, 1)

        @block.tensor
        def _(pe):
            mm = nc.tensor.matmul
            pe.wait_ge(s_const, 6)
            pe.wait_ge(s_cast, 2)
            pe.wait_ge(s_wsplit, 1)

            def head_scores(b, h, par):
                ps, n = ST_PS[h % 2], b * H + h
                q, k = QK[0:KK, par, 0, h, :], QK[0:KK, par, 1, h, :]
                if h == 0:
                    pe.wait_ge(s_mrow, 16 * (b + 1))
                at_least(pe, s_exp, n - 1)
                mm(ps[:, P:3 * P], k[:, P:T], q, start=True, stop=True, skip_group_check=True)
                mm(ps[:, 0:T], k[:, 0:P], q, start=True, stop=True, skip_group_check=True).then_inc(s_st, 1)

            def head_values(b, h):
                g, ps = h // GH, PV_PS[h // GH]
                if h % GH == 0:
                    pe.wait_ge(s_vp, (2 * b + g + 1) * NT)
                    at_least(pe, s_ev, 4 * b - 2 + 2 * g)
                    if g == 1:
                        at_least(pe, s_acc, b)
                pe.wait_ge(s_masked, b * H + h + 1)
                p = prob[:, h % 4, :]
                mm(ps[:, 0:T], vpad[:, h * P:(h + 1) * P], p[:, 0:T], start=(h % GH == 0), stop=False)
                mm(ps[:, P:T], vpad[:, (H + h) * P:(H + h + 1) * P], p[:, T:3 * P],
                   start=False, stop=(h % GH == GH - 1)).then_inc(s_pv, 1)

            def output_projection(b):
                pe.wait_ge(s_oT, b + 1)
                for j in range(NT):
                    ins = mm(PV_PS[1][:, j * P:(j + 1) * P], oT[:, j * P:(j + 1) * P], wo[:, :], start=True, stop=True)
                ins.then_inc(s_wo, 1)

            def turn_stacks(b, what):
                _, j, side, h0 = what
                rows = KK if side == "k" else KQ
                u, bank = UNITS.index(what), bank_of(what)
                if h0 == 0:
                    pe.wait_ge(s_dup[side], b * NT + j + 1)
                    pe.wait_ge(s_lo[side], b * NT + j + 1)
                at_least(pe, s_bfree[bank], b * B_FREES + u // 2)
                if u == 1:
                    at_least(pe, s_mT, b)
                for i in range(4):
                    ins = nc.tensor.transpose(B_PS[bank][0:rows, i * P:(i + 1) * P].bitcast(F32R),
                                              stk[side, j][:, h0 + i, 0:rows], identr[:, :])
                ins.then_inc(s_bfill, 1)

            def scores_for_max(b, what, par):
                h, u, bank = what[1], UNITS.index(what), bank_of(what)
                ps = B_PS[bank]
                q, k = QK[0:KQ, par, 0, h, :], QK[0:KQ, par, 1, h, :]
                last = max((("t", j, side, h // 4 * 4) for j in range(NT) for side in "qk"), key=UNITS.index)
                for i in range(2):
                    n = max(u // 2 if i == bank else 0, uses_until(last, i) if h % 4 == 0 else 0)
                    if n:
                        pe.wait_ge(s_bfree[i], b * B_FREES + n)
                mm(ps[:, 0:T], q[:, 0:P], k, start=True, stop=False, skip_group_check=True)
                mm(ps[:, P:3 * P], q[:, P:T], k, start=True, stop=False, skip_group_check=True)
                diag = ps[:, 0:3 * P].rearrange("p (a c) -> p a c", a=3)[:, 0:3:2, :]
                mm(diag, identb[:, :], mask_qk[:, :].unsqueeze(1).to_broadcast([P, 2, P]), start=False, stop=True,
                   skip_group_check=True).then_inc(s_bfill, 1)

            def turn_maxima(b):
                pe.wait_ge(s_nm, b + 1)
                pe.wait_ge(s_bfree[0], (b + 1) * B_FREES)
                for j in range(NT):
                    ins = nc.tensor.transpose(B_PS[0][0:2 * H, j * P:(j + 1) * P].bitcast(F32R),
                                              nhl[:, j, :, :].rearrange("p a h -> p (a h)"), identr[:, :])
                ins.then_inc(s_bfill, 1)

            def project(b, side, j, par):
                k0 = b * 4 + order_of(side, j)
                qrow, kvrow = qsT[:, j, :], ksT[:, j, :]
                xh, xl = (xhl[:, par, a, j * P:(j + 1) * P] for a in range(2))
                pe.wait_ge(s_smT, 2 * (b + 1))
                if side == "q":
                    for half in range(2):
                        bank = 1 - half
                        at_least(pe, s_pfree[bank], k0)
                        hs = slice(half * GH, (half + 1) * GH)
                        ps = banks[bank][:, 0:GH * D]
                        mm(ps, qrow, wqa[:, hs, :].rearrange("p h d -> p (h d)"), start=True, stop=False)
                        mm(ps, qrow, wqb[:, hs, :].rearrange("p h d -> p (h d)"), start=False, stop=True)\
                            .then_inc(s_pfill, 1)
                else:
                    pe.wait_ge(s_pfree[0], k0)
                    mm(banks[0][:, 0:2 * HD], kvrow, wkv[:, :], start=True, stop=True).then_inc(s_pfill, 1)
                    pe.wait_ge(s_pfree[1], k0)
                    mm(banks[1][:, :], xh, wkr[:, 0, :], start=True, stop=False)
                    mm(banks[1][:, :], xl, wkr[:, 0, :], start=False, stop=False)
                    mm(banks[1][:, :], xh, wkr[:, 1, :], start=False, stop=True).then_inc(s_pfill, 1)

            def values_and_projection(b, s):
                bb, h = values_of(b, s)
                if known(bb):
                    head_values(bb, h)
                if isinstance(b, int) and b == B and s == WO_STEP - 1:
                    for i in range(2):
                        pe.wait_ge(s_pfree[i], 4 * B)
                        pe.wait_ge(s_bfree[i], B_FREES * B)
                    pe.wait_ge(s_mT, B)
                    hidden(0, 0, 0)
                if s == WO_STEP and known(b - 1):
                    output_projection(b - 1)

            def turn(b, par):
                for s in range(STEPS):
                    bb, h = scores_of(b, s)
                    if known(bb):
                        head_scores(bb, h, par if s >= SHIFT else (par + 1) % 2)
                    if isinstance(b, int) and b == -1 and s == 0:
                        pe.wait_ge(s_wb, 16 * 2)
                        nc.tensor.transpose(banks[1][:, 0:NE * FC], braw, ident[0:NE * FC, 0:NE * FC]).then_inc(s_biasT, 1)
                        pe.wait_ge(s_bias, 1)
                    if s == MT_STEP and known(b):
                        turn_maxima(b)
                    for i, what in enumerate(UNITS_AT.get(s, ())):
                        if i == 1:
                            values_and_projection(b, s)
                        if known(b + 1):
                            if what[0] == "t":
                                turn_stacks(b + 1, what)
                            else:
                                scores_for_max(b + 1, what, (par + 1) % 2)
                    if len(UNITS_AT.get(s, ())) < 2:
                        values_and_projection(b, s)
                    if known(b + 2) and s in PROJ_AT:
                        project(b + 2, *PROJ_AT[s], par)
                    if known(b + 3):
                        if s == XT_STEP:
                            pe.wait_ge(s_xn, NT * (b + 4))
                            at_least(pe, s_pfree[0], 4 * (b + 3))
                            for j in range(NT):
                                ins = nc.tensor.transpose(banks[0][:, j * P:(j + 1) * P], xn[:, j, :], ident[:, :])
                            ins.then_inc(s_afill, 1)
                        if s == SM_STEP:
                            pe.wait_ge(s_xl, b + 4)
                            at_least(pe, s_pfree[1], 4 * (b + 3))
                            for j in range(NT):
                                for a in range(2):
                                    ins = mm(banks[1][:, j * T:(j + 1) * T],
                                             xhl[:, (par + 1) % 2, a, j * P:(j + 1) * P], wsm[:, :],
                                             start=(a == 0), stop=(a == 1))
                            ins.then_inc(s_afill, 1)
                        if s == QK_STEP:
                            pe.wait_ge(s_small, b + 4)
                            for j in range(NT):
                                nc.tensor.transpose(banks[0][:, j * P:(j + 1) * P].bitcast(F32R),
                                                    qs[:, j, :, :].rearrange("p a r -> p (a r)"), identr[:, :])
                            for j in range(NT):
                                ins = nc.tensor.transpose(banks[0][0:3 * RKV, (NT + j) * P:(NT + j + 1) * P].bitcast(F32R),
                                                          ks[:, j, :, :].rearrange("p a r -> p (a r)"), identr[:, :])
                            ins.then_inc(s_afill, 1)

            def hidden(g, n, e):
                m = n * NE + e
                if n == 0 and e in (0, E):
                    pe.wait_ge(s_w1l, E if e == 0 else NE)
                if e == 0:
                    pe.wait_ge(s_xc[n], (g + 1) * 16)
                for c in range(FC):
                    at_least(pe, s_act[c], g * (2 * NE) + m)
                    for i, (w, a) in enumerate(((0, 0), (0, 1), (1, 0))):
                        ins = mm(banks[c][:, :], w1_part(e, w, c * P, P), xc[n][:, a, :], start=(i == 0), stop=(i == 2))
                    ins.then_inc(s_l1, 1)

            run_turns(pe, turn)

            pe.wait_ge(s_exp, H * B)
            pe.wait_ge(s_ev, 4 * B)
            pe.wait_ge(s_acc, B)

            def spread(g, n, e):
                m = n * NE + e
                at_least(pe, s_repc, g * (2 * NE) + m)
                mm(banks[6][:, :], pick[:, e, :], cwT, start=True, stop=True).then_inc(s_rep, 1)

            def expert_out(g, n, e):
                m = n * NE + e
                M = g * (2 * NE) + m
                out_ps = banks[4 + m % 2]
                at_least(pe, s_yw, M - 1)
                for c in range(FC):
                    pe.wait_ge(s_ahi, M * FC + c + 1)
                    for w in range(2):
                        mm(out_ps[:, :], w2_part(e, w, c), aparts[:, m % 2, 0, c, :], start=(c == 0 and w == 0), stop=False)
                for c in range(FC):
                    pe.wait_ge(s_alo, M * FC + c + 1)
                    ins = mm(out_ps[:, :], w2_part(e, 0, c), aparts[:, m % 2, 1, c, :], start=False, stop=(c == FC - 1))
                ins.then_inc(s_l2, 1)

            def turn_sum(g, n):
                pe.wait_ge(s_ys, g * (2 * NE) + (n + 1) * NE)
                for i in range(4):
                    ins = nc.tensor.transpose(banks[7][:, i * P:(i + 1) * P], y_sum[:, i * P:(i + 1) * P], ident[:, :])
                ins.then_inc(s_tr, 1)

            pe.wait_ge(s_w2l, NE)
            pe.wait_ge(s_b2l, 1)
            pe.wait_ge(s_pick, 3)

            def chunks(g):
                for n in range(2):
                    if n or not isinstance(g, int):
                        hidden(g, n, 0)
                    pe.wait_ge(s_cw, g * 2 + n + 1)
                    at_least(pe, s_ys, g * (2 * NE) + n * NE - NE + 1)
                    for i in range(4):
                        ins = nc.tensor.transpose(banks[7][0:2 * NE, i * P:(i + 1) * P].bitcast(F32R), cwc[:, n, i, :], identr[:, :])
                    ins.then_inc(s_cwt, 1)
                    hidden(g, n, 1)
                    if n == 1 or not isinstance(g, int):
                        pe.wait_ge(s_cwe, g * 2 + n + 1)
                        turn_sum(g if n else g - 1, 1 - n)
                    for e in range(NE):
                        if 2 <= e + 1 < NE:
                            hidden(g, n, e + 1)
                        if e:
                            spread(g, n, e)
                        expert_out(g, n, e)
                        if e == 0:
                            pe.wait_ge(s_cwe, g * 2 + n + 1)
                            spread(g, n, 0)
                            if n == 1 or not isinstance(g, int):
                                pe.wait_ge(s_fin, g * 2 + n)
                            for a in range(2):
                                ins = mm(banks[7][:, :], b2p[:, a, :], cwT, start=(a == 0), stop=(a == 1))
                            ins.then_inc(s_b2, 1)

            run_chunks(pe, chunks)
            turn_sum(CHUNKS // 2 - 1, 1)


_INS = ['L0_attn_x', 'L0_attn_W_kv', 'L0_attn_g_kv', 'L0_attn_W_kdec', 'L0_attn_W_vdec', 'L0_attn_W_q',
        'L0_attn_W_qdec', 'L0_attn_W_krope', 'L0_attn_W_qrope', 'L0_attn_W_o', 'L0_ffn_Wg', 'L0_ffn_W1',
        'L0_ffn_b1', 'L0_ffn_W2', 'L0_ffn_b2', 'L0_ffn_Ws1', 'L0_ffn_bs1', 'L0_ffn_Ws2', 'L0_ffn_bs2']


def rope_table(np):
    inv_freq = 1.0 / 10000.0 ** (np.arange(0, DR, 2, dtype=np.float32) / DR)
    freqs = np.outer(np.arange(T, dtype=np.float32), inv_freq)
    cos, sin = np.cos(freqs), np.sin(freqs)
    return np.concatenate([np.ones((T, DC)), cos, cos, -sin, sin], -1).astype(np.float32)


def kernel(**inputs):
    import numpy as np
    import concourse.bacc as bacc
    from concourse.bass_utils import run_bass_kernel_spmd

    nc = bacc.Bacc("TRN2", target_bir_lowering=False, num_devices=1)
    arrays, args = {}, []
    for name in _INS:
        a = np.ascontiguousarray(inputs[name])
        arrays[f"in_{name}"] = a
        args.append(nc.dram_tensor(f"in_{name}", a.shape, mybir.dt.from_np(a.dtype), kind="ExternalInput").ap())
    table = rope_table(np)
    arrays["in_rope"] = table
    args.append(nc.dram_tensor("in_rope", table.shape, F32, kind="ExternalInput").ap())
    args.append(nc.dram_tensor("out", (B, T, C), F32, kind="ExternalOutput").ap())
    build(nc, *args)
    r = run_bass_kernel_spmd(nc, [arrays], core_ids=[0])
    return r.results[0]["out"]
```
